# Optimizing a Trainium2 kernel written in Bass

```python
import numpy as np
import jax
import jax.numpy as jnp

def _softmax(x, axis=-1):
    return jax.nn.softmax(x, axis=axis)

def _gelu(x):
    return jax.nn.gelu(x, approximate=True)

def _silu(x):
    return jax.nn.silu(x)

def _sigmoid(x):
    return jax.nn.sigmoid(x)

def _layernorm(x, axis=-1, eps=1e-05):
    m = jnp.mean(x, axis=axis, keepdims=True)
    v = jnp.var(x, axis=axis, keepdims=True)
    return (x - m) / jnp.sqrt(v + eps)

def _scatter_add(tgt, idx, src, axis=0):
    return tgt.at[idx].add(src)

def _segment_sum(src, seg, n):
    return jax.ops.segment_sum(src, seg, n)
kernel_name = 'mk_xattn_seq_d1_seqx_r4_59fe81'

def setup_inputs(seed: int=0):
    np.random.seed(seed)
    _w = jnp.asarray

    def _rec_inputs():
        import jax
        import jax.numpy as jnp
        _rk = jax.random.key(seed)
        x = -0.0002928 + 1 * jax.random.normal(jax.random.fold_in(_rk, 1), (2, 1024, 256), jnp.float32)
        _lenS = 1024 - jax.random.randint(jax.random.fold_in(_rk, 7), (2,), 0, max(1, 1024 // 4) + 1, jnp.int32)
        _lenS2 = 77 - jax.random.randint(jax.random.fold_in(_rk, 8), (2,), 0, max(1, 77 // 4) + 1, jnp.int32)
        _ctx_1024P = jax.random.normal(jax.random.fold_in(_rk, 11), (2, 16, 256), jnp.float32)
        _ctx_1024c = jax.random.dirichlet(jax.random.fold_in(_rk, 511), 0.3 * jnp.ones((16,), jnp.float32), (2, 77))
        _ctx_1024t = jnp.einsum('bsk,bkd->bsd', _ctx_1024c, _ctx_1024P)
        _ctx_1024t = _ctx_1024t * jax.lax.rsqrt(jnp.mean(jnp.square(_ctx_1024t)) + 1e-12) * 0.953939
        ctx_1024 = -1.39393e-06 + 0.999914 * (_ctx_1024t + 0.3 * jax.random.normal(jax.random.fold_in(_rk, 611), (2, 77, 256), jnp.float32))
        return (x, ctx_1024)
    x, ctx_1024 = _rec_inputs()

    def _L0_xattn_setup():
        import jax, jax.numpy as jnp
        import numpy as np
        B, T, TE, C, H = (2, 512, 512, 256, 16)
        DH = C // H
        EPS = 1e-05

        def _ln(x, g, b):
            mu = jnp.mean(x, axis=-1, keepdims=True)
            var = jnp.mean((x - mu) ** 2, axis=-1, keepdims=True)
            return (x - mu) * jax.lax.rsqrt(var + EPS) * g + b

        def _mha(xn, kv_src, Wq, bq, Wk, bk, Wv, bv, causal):
            q = jnp.einsum('btc,hcd->bhtd', xn, Wq) + bq[None, :, None, :]
            k = jnp.einsum('bsc,hcd->bhsd', kv_src, Wk) + bk[None, :, None, :]
            v = jnp.einsum('bsc,hcd->bhsd', kv_src, Wv) + bv[None, :, None, :]
            scale = DH ** (-0.5)
            scores = jnp.einsum('bhtd,bhsd->bhts', q, k) / scale
            if causal:
                Tq, Ts = (scores.shape[-2], scores.shape[-1])
                mask = jnp.tril(jnp.ones((Tq, Ts), dtype=bool))
                scores = jnp.where(mask[None, None], scores, -jnp.inf)
            attn = jax.nn.softmax(scores, axis=-1)
            out = jnp.einsum('bhts,bhsd->bhtd', attn, v)
            b_, h_, t_, d_ = out.shape
            return out.transpose(0, 2, 1, 3).reshape(b_, t_, h_ * d_)
        key = jax.random.key(seed)
        ks = jax.random.split(key, 24)
        s = 0.02
        d = {'x': jax.random.normal(ks[0], (B, T, C), jnp.float32), 'encoder_out': jax.random.normal(ks[1], (B, TE, C), jnp.float32), 'Wq_s': jax.random.normal(ks[2], (H, C, DH)) * s, 'bq_s': jnp.zeros((H, DH)), 'Wk_s': jax.random.normal(ks[3], (H, C, DH)) * s, 'bk_s': jnp.zeros((H, DH)), 'Wv_s': jax.random.normal(ks[4], (H, C, DH)) * s, 'bv_s': jnp.zeros((H, DH)), 'W1': jax.random.normal(ks[5], (C, C)) * s, 'b1': jnp.zeros((C,)), 'g1': jnp.ones((C,)), 'be1': jnp.zeros((C,)), 'Wq_c': jax.random.normal(ks[6], (H, C, DH)) * s, 'bq_c': jnp.zeros((H, DH)), 'Wk_c': jax.random.normal(ks[7], (H, C, DH)) * s, 'bk_c': jnp.zeros((H, DH)), 'Wv_c': jax.random.normal(ks[8], (H, C, DH)) * s, 'bv_c': jnp.zeros((H, DH)), 'W2': jax.random.normal(ks[9], (C, C)) * s, 'b2': jnp.zeros((C,)), 'g2': jnp.ones((C,)), 'be2': jnp.zeros((C,)), 'g3': jnp.ones((C,)), 'be3': jnp.zeros((C,)), 'Wf1': jax.random.normal(ks[10], (C, 4 * C)) * s, 'bf1': jnp.zeros((4 * C,)), 'Wf2': jax.random.normal(ks[11], (4 * C, C)) * s, 'bf2': jnp.zeros((C,))}
        return d
    _L0_xattn_all = _L0_xattn_setup()
    _L0_xattn_in = {k: v for k, v in _L0_xattn_all.items() if k in ('Wq_s', 'bq_s', 'Wk_s', 'bk_s', 'Wv_s', 'bv_s', 'W1', 'b1', 'g1', 'be1', 'Wq_c', 'bq_c', 'Wk_c', 'bk_c', 'Wv_c', 'bv_c', 'W2', 'b2', 'g2', 'be2', 'g3', 'be3', 'Wf1', 'bf1', 'Wf2', 'bf2')}
    del _L0_xattn_all
    return {'x': x, 'ctx_1024': ctx_1024, 'L0_xattn_Wq_s': _L0_xattn_in['Wq_s'], 'L0_xattn_bq_s': _L0_xattn_in['bq_s'], 'L0_xattn_Wk_s': _L0_xattn_in['Wk_s'], 'L0_xattn_bk_s': _L0_xattn_in['bk_s'], 'L0_xattn_Wv_s': _L0_xattn_in['Wv_s'], 'L0_xattn_bv_s': _L0_xattn_in['bv_s'], 'L0_xattn_W1': _L0_xattn_in['W1'], 'L0_xattn_b1': _L0_xattn_in['b1'], 'L0_xattn_g1': _L0_xattn_in['g1'], 'L0_xattn_be1': _L0_xattn_in['be1'], 'L0_xattn_Wq_c': _L0_xattn_in['Wq_c'], 'L0_xattn_bq_c': _L0_xattn_in['bq_c'], 'L0_xattn_Wk_c': _L0_xattn_in['Wk_c'], 'L0_xattn_bk_c': _L0_xattn_in['bk_c'], 'L0_xattn_Wv_c': _L0_xattn_in['Wv_c'], 'L0_xattn_bv_c': _L0_xattn_in['bv_c'], 'L0_xattn_W2': _L0_xattn_in['W2'], 'L0_xattn_b2': _L0_xattn_in['b2'], 'L0_xattn_g2': _L0_xattn_in['g2'], 'L0_xattn_be2': _L0_xattn_in['be2'], 'L0_xattn_g3': _L0_xattn_in['g3'], 'L0_xattn_be3': _L0_xattn_in['be3'], 'L0_xattn_Wf1': _L0_xattn_in['Wf1'], 'L0_xattn_bf1': _L0_xattn_in['bf1'], 'L0_xattn_Wf2': _L0_xattn_in['Wf2'], 'L0_xattn_bf2': _L0_xattn_in['bf2']}

def reference(x, ctx_1024, L0_xattn_Wq_s, L0_xattn_bq_s, L0_xattn_Wk_s, L0_xattn_bk_s, L0_xattn_Wv_s, L0_xattn_bv_s, L0_xattn_W1, L0_xattn_b1, L0_xattn_g1, L0_xattn_be1, L0_xattn_Wq_c, L0_xattn_bq_c, L0_xattn_Wk_c, L0_xattn_bk_c, L0_xattn_Wv_c, L0_xattn_bv_c, L0_xattn_W2, L0_xattn_b2, L0_xattn_g2, L0_xattn_be2, L0_xattn_g3, L0_xattn_be3, L0_xattn_Wf1, L0_xattn_bf1, L0_xattn_Wf2, L0_xattn_bf2):
    import jax
    import jax.numpy as jnp

    def _L0_xattn_ref(x, encoder_out, Wq_s, bq_s, Wk_s, bk_s, Wv_s, bv_s, W1, b1, g1, be1, Wq_c, bq_c, Wk_c, bk_c, Wv_c, bv_c, W2, b2, g2, be2, g3, be3, Wf1, bf1, Wf2, bf2):
        import jax, jax.numpy as jnp
        import numpy as np
        B, T, TE, C, H = (2, 512, 512, 256, 16)
        DH = C // H
        EPS = 1e-05

        def _ln(x, g, b):
            mu = jnp.mean(x, axis=-1, keepdims=True)
            var = jnp.mean((x - mu) ** 2, axis=-1, keepdims=True)
            return (x - mu) * jax.lax.rsqrt(var + EPS) * g + b

        def _mha(xn, kv_src, Wq, bq, Wk, bk, Wv, bv, causal):
            q = jnp.einsum('btc,hcd->bhtd', xn, Wq) + bq[None, :, None, :]
            k = jnp.einsum('bsc,hcd->bhsd', kv_src, Wk) + bk[None, :, None, :]
            v = jnp.einsum('bsc,hcd->bhsd', kv_src, Wv) + bv[None, :, None, :]
            scale = DH ** (-0.5)
            scores = jnp.einsum('bhtd,bhsd->bhts', q, k) / scale
            if causal:
                Tq, Ts = (scores.shape[-2], scores.shape[-1])
                mask = jnp.tril(jnp.ones((Tq, Ts), dtype=bool))
                scores = jnp.where(mask[None, None], scores, -jnp.inf)
            attn = jax.nn.softmax(scores, axis=-1)
            out = jnp.einsum('bhts,bhsd->bhtd', attn, v)
            b_, h_, t_, d_ = out.shape
            return out.transpose(0, 2, 1, 3).reshape(b_, t_, h_ * d_)
        xn1 = _ln(x, g1, be1)
        sa = _mha(xn1, xn1, Wq_s, bq_s, Wk_s, bk_s, Wv_s, bv_s, causal=True)
        x = x + (sa @ W1 + b1)
        xn2 = _ln(x, g2, be2)
        ca = _mha(xn2, encoder_out, Wq_c, bq_c, Wk_c, bk_c, Wv_c, bv_c, causal=False)
        x = x + (ca @ W2 + b2)
        xn3 = _ln(x, g3, be3)
        ff = jax.nn.relu(xn3 @ Wf1 + bf1) @ Wf2 + bf2
        return x + ff
    x = _L0_xattn_ref(x, ctx_1024, L0_xattn_Wq_s, L0_xattn_bq_s, L0_xattn_Wk_s, L0_xattn_bk_s, L0_xattn_Wv_s, L0_xattn_bv_s, L0_xattn_W1, L0_xattn_b1, L0_xattn_g1, L0_xattn_be1, L0_xattn_Wq_c, L0_xattn_bq_c, L0_xattn_Wk_c, L0_xattn_bk_c, L0_xattn_Wv_c, L0_xattn_bv_c, L0_xattn_W2, L0_xattn_b2, L0_xattn_g2, L0_xattn_be2, L0_xattn_g3, L0_xattn_be3, L0_xattn_Wf1, L0_xattn_bf1, L0_xattn_Wf2, L0_xattn_bf2)
    return x

_drawn_inputs = setup_inputs


def setup_inputs(seed=0):
    import zlib

    import numpy as np

    out = dict(_drawn_inputs(seed))
    spreads = {'L0_xattn_bq_s': (0.0, 0.8),
     'L0_xattn_bk_s': (0.0, 0.8),
     'L0_xattn_bv_s': (0.0, 0.1),
     'L0_xattn_b1': (0.0, 0.1),
     'L0_xattn_g1': (1.0, 0.6),
     'L0_xattn_be1': (0.0, 0.743),
     'L0_xattn_bq_c': (0.0, 0.41),
     'L0_xattn_bk_c': (0.0, 0.8),
     'L0_xattn_bv_c': (0.0, 0.273),
     'L0_xattn_b2': (0.0, 0.1),
     'L0_xattn_g2': (1.0, 0.6),
     'L0_xattn_be2': (0.0, 0.8),
     'L0_xattn_g3': (1.0, 0.555),
     'L0_xattn_be3': (0.0, 0.571),
     'L0_xattn_bf1': (0.0, 0.1),
     'L0_xattn_bf2': (0.0, 0.1)}
    factors = {}
    for name, (base, spread) in spreads.items():
        noise = np.random.default_rng([zlib.crc32(name.encode()), seed]).standard_normal(out[name].shape)
        drawn = base * np.exp(spread * noise) if base else spread * noise
        out[name] = jnp.asarray(drawn.astype(out[name].dtype))
    for name, factor in factors.items():
        out[name] = (out[name] * factor).astype(out[name].dtype)
    return out
```

```python
from contextlib import ExitStack

import concourse.bass as bass
from concourse import mybir

ALU = mybir.AluOpType
ACT = mybir.ActivationFunctionType
AX = mybir.AxisListType
F32 = mybir.dt.float32
BF16 = mybir.dt.bfloat16

P = 128
B, T, C, H, D = 2, 1024, 256, 16, 16
S_CTX = 77
FF = 4 * C
EPS = 1e-5
KC = C // P
CHUNK = 512
CT = CHUNK // P
NCH = B * T // CHUNK
TILES = T // P
GH = 4
NG = B * H // GH
GW = GH * D
PARTS = 3
QP = [0, 0, 0, 1, 1, 2]
KP = [0, 1, 2, 0, 1, 0]
ROWS = D * len(QP)
ROWS_S = ROWS + PARTS
SCALE = float(D) ** 0.5
NEG = -1e30
NB = 3

BQ_S, BK_S, BQ_C, BK_C, G1, BE1, G2, BE2, G3, BE3, BF1 = 0, 2, 4, 6, 8, 10, 12, 14, 16, 18, 20
NCOLS = 20 + FF // P
BV_S, B1, BV_C, B2, BF2 = range(5)
W1, WQ_C, W2 = 0, C, 2 * C


class Attention:

    def __init__(self, causal, keys):
        self.causal, self.keys = causal, keys
        self.kt = -(-keys // P)
        if causal:
            groups = [[0], [1], [2], [3], [4, 5], [6, 7]]
        else:
            groups = [[0]]
        self.steps = []
        for tiles in groups:
            off, pieces = 0, []
            for i in tiles:
                w = T - i * P if causal else T
                pieces.append((i, T - w, w, off))
                off += w
            self.steps.append((pieces, off))
        self.chunks = []
        for t in range(TILES):
            keys_t = (t + 1) * P if causal else keys
            for s in range(0, keys_t, 512):
                w = min(512, keys_t - s)
                at_once = min(512 // w, GH)
                if t == 0:
                    at_once = GH // 2
                for h in range(0, GH, at_once):
                    self.chunks.append((t, h, at_once, s, w))
        self.second = [t for t in range(TILES) if causal and t >= 4]
        self.n_steps = len(self.steps)
        self.units = GH * self.n_steps
        self.m_max = len(self.chunks) + 1
        self.m_all = self.m_max + 2
        assert self.m_max % 2 == 0
        self.masks = 8 if causal else 0
        last = 19 if causal else GH
        self.until = [min(len(self.chunks), -(-len(self.chunks) * (u + 1) // last)) for u in range(self.units)]
        self.kp = P if causal else keys

    def m_base(self, g):
        if isinstance(g, int):
            return self.m_max if g == 0 else 2 * self.m_max + self.m_all * (g - 1) if g < NG \
                else 2 * self.m_max + self.m_all * (NG - 2) + 2
        return g * self.m_all + (2 * self.m_max - self.m_all)

    def masks_before(self, ui):
        return sum(len(self.steps[u][0]) for u in range(ui))


SELF = Attention(True, T)
CROSS = Attention(False, S_CTX)


def at_least(eng, sem, value):
    if not isinstance(value, int) or value > 0:
        eng.wait_ge(sem, value)


def build(nc, x, w_qkv, w_ctx, w_mid, w_f1, w_f2, ctx_t, cols, rows, out):
    x_d = x.rearrange("b t c -> (b t) c").rearrange("(n p) c -> p n c", p=P)
    out_d = out.rearrange("b t c -> (b t) c").rearrange("(n p) c -> p n c", p=P)
    q_dram = nc.dram_tensor("q_parts", (PARTS, NG, GW, T), BF16).ap()
    k_dram = nc.dram_tensor("k_parts", (PARTS, NG, GW, T), BF16).ap()
    qc_dram = nc.dram_tensor("qc_parts", (PARTS, NG, GW, T), BF16).ap()
    kc_dram = nc.dram_tensor("kc_parts", (PARTS, NG, GW, S_CTX), BF16).ap()

    with ExitStack() as ctx:
        def sb(name, shape, dt=F32):
            return ctx.enter_context(nc.sbuf_tensor(name, shape, dt))

        def sem(name):
            return ctx.enter_context(nc.semaphore(name))

        xs = sb("xs", [P, NCH * CT, C])
        wqkv = sb("wqkv", [P, KC, 3 * C])
        wctx = sb("wctx", [P, KC, 2 * C])
        ctxt = sb("ctxt", [P, KC, B * S_CTX])
        wmid = sb("wmid", [P, KC, 3 * C])
        col = sb("col", [P, NCOLS])
        row = sb("row", [P, 5, C])
        identf = sb("identf", [P, P])
        identb = sb("identb", [P, P], BF16)
        maskb = sb("maskb", [P, P], BF16)
        neghalf = sb("neghalf", [P, CT])
        heads_out = sb("heads_out", [P, NG // 2, TILES, 2 * GW])
        arena_v = sb("arena_v", [P, NG * TILES * GW])
        v_self = arena_v[:, :].rearrange("p (g i c) -> p g i c", g=NG, i=TILES)
        wf1 = arena_v[:, 0:KC * FF].rearrange("p (k n) -> p k n", k=KC)
        wf2 = arena_v[:, KC * FF:2 * KC * FF].rearrange("p (k n) -> p k n", k=FF // P)
        v_ctx = sb("v_ctx", [S_CTX, NG, GW])
        q_stack = sb("q_stack", [ROWS_S, NB, GH, T], BF16)
        k_stack = sb("k_stack", [ROWS_S, NB, GH, T], BF16)
        v_group = sb("v_group", [P, NB, TILES, GH, 32])
        arena_p = sb("arena_p", [P, 3 * GH * T])
        probs = arena_p[:, :].rearrange("p (s h t) -> p s h t", s=3, h=GH)
        out_t = sb("out_t", [P, T])
        max_a = sb("max_a", [P, GH, TILES])
        max_b = sb("max_b", [P, GH, 4])
        neg_m = sb("neg_m", [P, GH * TILES])
        neg_r = sb("neg_r", [P, GH * TILES])
        shift = sb("shift", [P, PARTS, GH * TILES], BF16)
        shift_t = sb("shift_t", [PARTS * GH * TILES, P], BF16)
        recip = sb("recip", [P, 2, 16])
        at = [0]

        def scratch(*shape):
            n = 1
            for s in shape:
                n *= s
            a = arena_p[:, at[0]:at[0] + n]
            at[0] += n
            names = "abcd"[:len(shape)]
            if len(shape) == 1:
                return a
            return a.rearrange("p (" + " ".join(names) + ") -> p " + " ".join(names),
                               **{k: s for k, s in zip(names, shape)})
        xn = scratch(2, CT, C)
        xn_t = scratch(2, KC, CHUNK)
        full = scratch(2, CHUNK)
        rest = scratch(2, CHUNK)
        parts = sb("parts", [P, 4, PARTS, CHUNK], BF16)
        ho_t = out_t[:, :].rearrange("p (k t) -> p k t", k=KC)
        hid_t = scratch(FF // P, CHUNK)
        stats = sb("stats", [P, CT, 6])
        mean_var = sb("mean_var", [P, 2, CT, 2])
        veps = sb("veps", [P, 2, CT])
        rstd = sb("rstd", [P, 2, CT])

        ps = ctx.enter_context(nc.psum_tensor("ps", [P, 8, 512], F32))
        acc = ps[:, 6:8, :].rearrange("p b (j c) -> p (b j) c", c=C)
        score_region = [ps[:, 0:2, :].rearrange("p b n -> p (b n)"), ps[:, 2:4, :].rearrange("p b n -> p (b n)")]
        out_region = ps[:, 4:6, :].rearrange("p b n -> p (b n)")

        x_in = [sem(f"x_in{n}") for n in range(NCH)]
        wqkv_in, col_in, row_in, ctx_in, mid_in, ff_in = (sem(n) for n in
            ("wqkv_in", "col_in", "row_in", "ctx_in", "mid_in", "ff_in"))
        consts = sem("consts")
        ln_stats, ln_var, ln_veps, ln_rstd, ln_done = (sem(n) for n in
            ("ln_stats", "ln_var", "ln_veps", "ln_rstd", "ln_done"))
        bias_added = sem("bias_added")
        tp_full, tp_read = sem("tp_full"), sem("tp_read")
        ring_full, ring_read = sem("ring_full"), sem("ring_read")
        acc_full, acc_read = sem("acc_full"), sem("acc_read")
        split_a, split_v = sem("split_a"), sem("split_v")
        parts_out = [sem(f"parts_out{s}") for s in range(4)]
        hid_done, out_done = sem("hid_done"), sem("out_done")

        class Sems:
            def __init__(self, pre):
                s = lambda name: sem(f"{pre}_{name}")
                self.q_in = [s(f"q_in{p}") for p in range(NB)]
                self.shift_in = [s(f"shift_in{p}") for p in range(NB)]
                self.v_set = s("v_set")
                self.max_full, self.max_read = s("max_full"), s("max_read")
                self.maxima = s("maxima")
                self.shift_step = s("shift_step")
                self.scores, self.exps = s("scores"), s("exps")
                self.masked = s("masked")
                self.pv = s("pv")
                self.out_copied = s("out_copied")
                self.recips = s("recips")
        S1, S2 = Sems("self"), Sems("cross")

        t_order = [("x", k) for k in range(NCH)]
        for base in (NCH, 2 * NCH):
            t_order.append(("o", base))
            for n in range(NCH + (base == NCH)):
                if n + 1 < NCH:
                    t_order.append(("o", base + n + 1))
                if base == NCH and n >= 1:
                    t_order.append(("x", base + n - 1))
                if base == 2 * NCH:
                    t_order.append(("x", base + n))
        t_at = {key: i for i, key in enumerate(t_order)}
        a_order = [("v", n) for n in range(NCH)] + [("vc", 0)] + [("w", NCH + n) for n in range(NCH)]
        for n in range(NCH):
            a_order.append(("w", 2 * NCH + n))
            if n:
                a_order.append(("f", n - 1))
        a_order.append(("f", NCH - 1))
        a_at = {key: i for i, key in enumerate(a_order)}
        U_KC, U_QC, U_H = 4 * NCH, 4 * NCH + 2, 4 * NCH + 2 + 2 * NCH

        def split_unit(u):
            if u < U_KC:
                n, s = divmod(u, 4)
                dst, c0 = (q_dram, BQ_S) if s < 2 else (k_dram, BK_S)
                hh = s % 2
            elif u < U_QC:
                hh = u - U_KC
                d = [kc_dram[:, 4 * b + 2 * hh:4 * b + 2 * hh + 2, :, :] for b in range(B)]
                return B * S_CTX, BK_C + hh, [(a.rearrange("p g r t -> (g r) p t"), b * S_CTX, S_CTX)
                                              for b, a in enumerate(d)]
            else:
                n, hh = divmod(u - U_QC, 2)
                dst, c0 = qc_dram, BQ_C
            b, t0 = n // 2, (n % 2) * CHUNK
            a = dst[:, 4 * b + 2 * hh:4 * b + 2 * hh + 2, :, t0:t0 + CHUNK]
            return CHUNK, c0 + hh, [(a.rearrange("p g r t -> (g r) p t"), 0, CHUNK)]

        def parts_landed(u):
            return 16 * sum(2 if U_KC <= v < U_QC else 1 for v in range(u % 4, u + 1, 4))

        block = ctx.enter_context(nc.Block())

        @block.sync
        def _(sp):
            sp.dma_start(xs[:, 0:CT, :], x_d[:, 0:CT, :]).then_inc(x_in[0], 16)
            sp.dma_start(col[:, :], cols).then_inc(col_in, 16)
            sp.dma_start(wqkv[:, :, :], w_qkv.rearrange("(k p) n -> p k n", p=P)).then_inc(wqkv_in, 16)
            for n in range(1, NCH):
                sp.dma_start(xs[:, n * CT:(n + 1) * CT, :], x_d[:, n * CT:(n + 1) * CT, :]).then_inc(x_in[n], 16)
                if n == 1:
                    sp.dma_start(row[:, :, :], rows.rearrange("(o r) c -> o r c", o=1).to_broadcast([P, 5, C]))\
                        .then_inc(row_in, 16)
            sp.dma_start(wctx[:, :, :], w_ctx.rearrange("(k p) n -> p k n", p=P)).then_inc(ctx_in, 16)
            sp.dma_start(ctxt[:, :, :], ctx_t.rearrange("(k p) n -> p k n", p=P)).then_inc(ctx_in, 16)
            sp.dma_start(wmid[:, :, :], w_mid.rearrange("(k p) n -> p k n", p=P)).then_inc(mid_in, 16)

            def store_parts(u):
                width, _, dsts = split_unit(u)
                sp.wait_ge(split_v, 3 * u + 3)
                for dst, c0, w in dsts:
                    sp.dma_start(dst, parts[:, u % 4, :, c0:c0 + w]).then_inc(parts_out[u % 4], 16)

            def load_stacks(a, s, g, par, q_src, k_src):
                at_least(sp, s.scores, a.units * (g - (NB - 1)))
                for src, dst, which, n in ((q_src, q_stack, QP, T), (k_src, k_stack, KP, a.keys)):
                    for blk, part in enumerate(which):
                        one = src[part, bass.ds(g, 1), :, :] if not isinstance(g, int) else src[part, g:g + 1, :, :]
                        sp.dma_start(dst[blk * D:(blk + 1) * D, par, :, 0:n],
                                     one.rearrange("o (h d) t -> d (o h) t", d=D)).then_inc(s.q_in[par], 16)

            def load_shift(a, s, g, par):
                sp.wait_ge(s.max_read, a.m_base(g - 1) + a.m_max if g else a.m_max)
                for k in range(PARTS):
                    n = GH * TILES
                    sp.dma_start(q_stack[ROWS + k:ROWS + k + 1, par, :, :].rearrange("o h (i t) -> o (h i) t", t=P),
                                 shift_t[k * n:(k + 1) * n, :]).then_inc(s.shift_in[par], 16)

            def attention(a, s, q_src, k_src):
                load_stacks(a, s, 0, 0, q_src, k_src)
                load_stacks(a, s, 1, 1, q_src, k_src)
                load_shift(a, s, 0, 0)

                def interval(g, par):
                    if not isinstance(g, int) or g + 2 < NG:
                        load_stacks(a, s, g + 2, (par + 2) % NB, q_src, k_src)
                    if not isinstance(g, int) or g + 1 < NG:
                        load_shift(a, s, g + 1, (par + 1) % NB)
                interval(0, 0)
                for g in range(1, NG):
                    interval(g, g % NB)

            for u in range(U_QC):
                store_parts(u)
            for slot in range(4):
                last = max(u for u in range(U_QC) if u % 4 == slot)
                sp.wait_ge(parts_out[slot], parts_landed(last))
            attention(SELF, S1, q_dram, k_dram)
            sp.wait_ge(S1.v_set, NG)
            sp.dma_start(wf1, w_f1.rearrange("(k p) n -> p k n", p=P)).then_inc(ff_in, 16)
            sp.dma_start(wf2, w_f2.rearrange("(k p) n -> p k n", p=P)).then_inc(ff_in, 16)
            for u in range(U_QC, U_H):
                store_parts(u)
            for slot in range(4):
                last = max(u for u in range(U_H) if u % 4 == slot)
                sp.wait_ge(parts_out[slot], parts_landed(last))
            attention(CROSS, S2, qc_dram, kc_dram)
            for n in range(NCH):
                for half in range(2):
                    sp.wait_ge(acc_read, 2 * a_at["f", n] + half + 1)
                    t0 = n * CT + 2 * half
                    sp.dma_start(out_d[:, t0:t0 + 2, :], xs[:, t0:t0 + 2, :]).then_inc(out_done, 16)
            sp.wait_ge(out_done, 16 * 2 * NCH)

        @block.gpsimd
        def _(pool):
            c = [0]

            def made(ins, n=1):
                ins.then_inc(consts, 1)
                c[0] += 1
            made(pool.memset(identf[:, :], 0.0))
            made(pool.memset(identb[:, :], 0.0))
            made(pool.memset(maskb[:, :], 0.0))
            made(pool.memset(neghalf[:, :], -0.5))
            pool.wait_ge(consts, 4)
            for m in (identf, identb):
                made(pool.affine_select(out=m[:, :], in_=m[:, :], compare_op=ALU.not_equal, fill=1.0, base=0,
                                        pattern=[[-1, P]], channel_multiplier=1))
            made(pool.affine_select(out=maskb[:, :], in_=maskb[:, :], compare_op=ALU.is_ge, fill=NEG, base=0,
                                    pattern=[[-1, P]], channel_multiplier=1))

            def ln_root(k):
                pool.wait_ge(ln_var, k + 1)
                pool.tensor_scalar(veps[:, k % 2, :], mean_var[:, k % 2, :, 1], EPS, None, ALU.add)\
                    .then_inc(ln_veps, 1)
                pool.wait_ge(ln_veps, k + 1)
                pool.tensor_tensor(rstd[:, k % 2, :], veps[:, k % 2, :], neghalf[:, :], ALU.pow)\
                    .then_inc(ln_rstd, 1)

            def add_bias(k):
                n = k % NCH
                r = (B1, B2, BF2)[k // NCH]
                pool.wait_ge(ln_done, CT * (k + 1))
                if k == 0:
                    pool.wait_ge(row_in, 16)
                for j in range(CT):
                    xt = xs[:, n * CT + j, :]
                    ins = pool.tensor_tensor(xt, xt, row[:, r, :], ALU.add)
                ins.then_inc(bias_added, 1)

            def attention(a, s, v_src):
                def set_v(g, par):
                    at_least(pool, s.pv, a.n_steps * (g - (NB - 1)))
                    src = v_src[:, bass.ds(g, 1), :] if a is CROSS else v_src[:, bass.ds(g, 1), :, :]
                    if a is CROSS:
                        src = src.rearrange("p o (h d) -> p o h d", d=D)
                        dst = v_group[0:a.kp, par, 0:1, :, 0:D]
                    else:
                        src = src.rearrange("p o i (h d) -> p (o i) h d", d=D)
                        dst = v_group[:, par, :, :, 0:D]
                    pool.tensor_copy(dst, src).then_inc(s.v_set, 1)

                def split_shift(g):
                    pool.wait_ge(s.maxima, g + 1)
                    m = max_a[:, :, :].rearrange("p h i -> p (h i)")
                    base = 5 * g
                    pool.tensor_scalar(neg_m[:, :], m, -1.0, None, ALU.mult).then_inc(s.shift_step, 1)
                    pool.wait_ge(s.shift_step, base + 1)
                    pool.tensor_copy(shift[:, 0, :], neg_m[:, :]).then_inc(s.shift_step, 1)
                    pool.wait_ge(s.shift_step, base + 2)
                    pool.tensor_tensor(neg_r[:, :], neg_m[:, :], shift[:, 0, :], ALU.subtract)\
                        .then_inc(s.shift_step, 1)
                    pool.wait_ge(s.shift_step, base + 3)
                    pool.tensor_copy(shift[:, 1, :], neg_r[:, :]).then_inc(s.shift_step, 1)
                    pool.wait_ge(s.shift_step, base + 4)
                    pool.tensor_tensor(shift[:, 2, :], neg_r[:, :], shift[:, 1, :], ALU.subtract)\
                        .then_inc(s.shift_step, 1)

                def mask(g, ui):
                    pieces, _ = a.steps[ui]
                    slot = ui % 3
                    pool.wait_ge(s.exps, a.units * g + GH * (ui + 1))
                    for i, q0, w, off in pieces:
                        blk = probs[:, slot, :, off:off + P]
                        pool.affine_select(out=blk, in_=blk, compare_op=ALU.is_ge, fill=0.0, base=0,
                                           pattern=[[0, GH], [1, P]], channel_multiplier=-1).then_inc(s.masked, 1)

                set_v(0, 0)
                split_shift(0)
                for g in range(NG):
                    if g + 1 < NG:
                        set_v(g + 1, (g + 1) % NB)
                    for ui in range(a.n_steps):
                        if ui == a.n_steps - 2 and a.causal and g + 1 < NG:
                            split_shift(g + 1)
                        if a.causal:
                            mask(g, ui)
                    if not a.causal and g + 1 < NG:
                        split_shift(g + 1)

            made(pool.memset(v_group[:, :, :, :, D:32], 1.0))
            ln_root(0)
            for k in range(1, NCH):
                ln_root(k)
                add_bias(k - 1)
            add_bias(NCH - 1)
            pool.wait_ge(bias_added, NCH)
            made(pool.memset(k_stack[ROWS:ROWS_S, :, :, :], 1.0))
            pool.wait_ge(consts, 9)
            pool.wait_ge(acc_read, 2 * a_at["vc", 0] + 2)
            attention(SELF, S1, v_self)
            for k in range(NCH, 2 * NCH):
                ln_root(k)
                add_bias(k)
            attention(CROSS, S2, v_ctx)
            for k in range(2 * NCH, 3 * NCH):
                ln_root(k)
                add_bias(k)

        @block.scalar
        def _(act):
            def copy_norm(k):
                i, p = t_at["x", k], k % 2
                gcol, bcol = ((G1, BE1), (G2, BE2), (G3, BE3))[k // NCH]
                for kc in range(KC):
                    act.wait_ge(tp_full, 2 * i + kc + 1)
                    if kc == 0 and 2 <= k < NCH:
                        act.wait_ge(acc_full, 2 * a_at["v", k - 2] + 2)
                    if kc == 0 and NCH + 2 <= k < 2 * NCH:
                        act.wait_ge(ring_full, U_QC + 2 * (k - NCH - 2) + 2)
                    if kc == 0 and 2 * NCH + 2 <= k:
                        act.wait_ge(ring_full, U_H + 8 * (k - 2 * NCH - 2) + 8)
                    nc.scalar.activation(xn_t[:, p, kc, :], ps[:, kc, :], ACT.Identity,
                                         scale=col[:, gcol + kc:gcol + kc + 1],
                                         bias=col[:, bcol + kc:bcol + kc + 1]).then_inc(tp_read, 1)

            def copy_heads(k):
                i = t_at["o", k]
                for kc in range(KC):
                    act.wait_ge(tp_full, 2 * i + kc + 1)
                    if kc == 0 and k % NCH:
                        act.wait_ge(acc_full, 2 * a_at["w", k - 1] + 2)
                    nc.scalar.activation(ho_t[:, kc, :], ps[:, kc, :], ACT.Copy).then_inc(tp_read, 1)

            def split(u):
                width, c, _ = split_unit(u)
                src = ps[:, 2 + u % 4, 0:width]
                act.wait_ge(ring_full, u + 1)
                at_least(act, split_v, 3 * (u - 2) + 3)
                nc.scalar.activation(full[:, u % 2, 0:width], src, ACT.Identity, bias=col[:, c:c + 1])\
                    .then_inc(split_a, 1)
                if u >= 4:
                    act.wait_ge(parts_out[u % 4], parts_landed(u - 4))
                nc.scalar.activation(parts[:, u % 4, 0, 0:width], src, ACT.Identity, bias=col[:, c:c + 1])\
                    .then_inc(split_a, 1)

            def attention(a, s):
                def exps(g, par, ui):
                    pieces, width = a.steps[ui]
                    slot = (a.n_steps * par + ui) % 3
                    at_least(act, s.pv, a.n_steps * g + ui - 2)
                    for h in range(GH):
                        act.wait_ge(s.scores, a.units * g + GH * ui + h + 1)
                        nc.scalar.activation(probs[0:a.kp, slot, h, 0:width],
                                             score_region[h % 2][0:a.kp, 0:width], ACT.Exp, scale=SCALE)\
                            .then_inc(s.exps, 1)

                def copy_out(g):
                    act.wait_ge(s.pv, a.n_steps * (g + 1))
                    at_least(act, s.max_full, a.m_base(g) + a.m_all - (0 if g + 1 < NG else a.m_max) if g else 0)
                    nc.scalar.activation(out_t[:, :], out_region, ACT.Copy).then_inc(s.out_copied, 1)

                for g in range(NG):
                    for ui in range(a.n_steps):
                        exps(g, g % NB, ui)
                        if ui == 0 and g:
                            copy_out(g - 1)
                copy_out(NG - 1)

            act.wait_ge(col_in, 16)
            for k in range(NCH):
                copy_norm(k)
                if k:
                    for u in range(4):
                        split(4 * (k - 1) + u)
            for u in range(4):
                split(4 * (NCH - 1) + u)
            for u in range(2):
                split(U_KC + u)
            act.wait_ge(split_v, 3 * U_QC)
            act.wait_ge(acc_full, 2 * a_at["vc", 0] + 2)
            act.wait_ge(tp_full, 2 * NCH)
            attention(SELF, S1)
            act.wait_ge(S1.max_full, SELF.m_base(NG) + 2)
            copy_heads(NCH)
            for n in range(NCH + 1):
                if n + 1 < NCH:
                    copy_heads(NCH + n + 1)
                if n:
                    copy_norm(NCH + n - 1)
                    for u in range(2):
                        split(U_QC + 2 * (n - 1) + u)
            act.wait_ge(split_v, 3 * U_H)
            act.wait_ge(ring_full, U_H)
            attention(CROSS, S2)
            act.wait_ge(S2.max_full, CROSS.m_base(NG) + 2)
            copy_heads(2 * NCH)
            for n in range(NCH):
                if n + 1 < NCH:
                    copy_heads(2 * NCH + n + 1)
                copy_norm(2 * NCH + n)
                if n:
                    act.wait_ge(acc_full, 2 * a_at["f", n - 1] + 2)
                for f in range(FF // P):
                    u = U_H + n * (FF // P) + f
                    act.wait_ge(ring_full, u + 1)
                    nc.scalar.activation(hid_t[:, f, :], ps[:, 2 + u % 4, :], ACT.Relu,
                                         bias=col[:, BF1 + f:BF1 + f + 1]).then_inc(hid_done, 1)

        @block.tensor
        def _(pe):
            def turn_norm(k):
                i, p = t_at["x", k], k % 2
                pe.wait_ge(ln_done, CT * (k + 1))
                for kc in range(KC):
                    at_least(pe, tp_read, 2 * (i - 1) + kc + 1)
                    for j in range(CT):
                        ins = nc.tensor.transpose(ps[:, kc, j * P:(j + 1) * P], xn[:, p, j, kc * P:(kc + 1) * P],
                                                  identf[:, :])
                    ins.then_inc(tp_full, 1)

            def turn_heads(k):
                i, n = t_at["o", k], k % NCH
                b, i0 = n // 2, (n % 2) * CT
                for kc in range(KC):
                    at_least(pe, tp_read, 2 * (i - 1) + kc + 1)
                    for j in range(CT):
                        ins = nc.tensor.transpose(ps[:, kc, j * P:(j + 1) * P],
                                                  heads_out[:, KC * b + kc, i0 + j, :], identf[:, :])
                    ins.then_inc(tp_full, 1)

            def ring_free(u):
                if u - 4 >= U_H:
                    pe.wait_ge(hid_done, u - 4 - U_H + 1)
                elif u >= 4:
                    pe.wait_ge(split_a, 2 * (u - 4) + 2)

            def project(u, k, weights, rhs, width):
                ring_free(u)
                for kc in range(KC):
                    ins = nc.tensor.matmul(ps[:, 2 + u % 4, 0:width], weights(kc), rhs(kc),
                                           start=(kc == 0), stop=(kc == KC - 1))
                ins.then_inc(ring_full, 1)

            def rows_product(key, lhs_t, rhs, n_k):
                i = a_at[key]
                for half in range(2):
                    at_least(pe, acc_read, 2 * (i - 1) + half + 1)
                    for j in (2 * half, 2 * half + 1):
                        for k in range(n_k):
                            ins = nc.tensor.matmul(acc[:, j, :], lhs_t(k, j), rhs(k), start=(k == 0),
                                                   stop=(k == n_k - 1))
                    ins.then_inc(acc_full, 1)

            def qkv(n):
                p = n % 2
                if n == 0:
                    pe.wait_ge(wqkv_in, 16)
                pe.wait_ge(tp_read, 2 * t_at["x", n] + 2)
                for s in range(4):
                    project(4 * n + s, n, lambda kc: wqkv[:, kc, s * P:(s + 1) * P],
                            lambda kc: xn_t[:, p, kc, :], CHUNK)
                rows_product(("v", n), lambda k, j: xn_t[:, p, k, j * P:(j + 1) * P],
                             lambda k: wqkv[:, k, 2 * C:3 * C], KC)

            def context():
                pe.wait_ge(ctx_in, 32)
                for hh in range(2):
                    project(U_KC + hh, 0, lambda kc: wctx[:, kc, hh * P:(hh + 1) * P], lambda kc: ctxt[:, kc, :],
                            B * S_CTX)
                i = a_at["vc", 0]
                pe.wait_ge(acc_read, 2 * i)
                for b in range(B):
                    for kc in range(KC):
                        ins = nc.tensor.matmul(acc[0:S_CTX, 2 * b, :], ctxt[:, kc, b * S_CTX:(b + 1) * S_CTX],
                                               wctx[:, kc, C:2 * C], start=(kc == 0), stop=(kc == KC - 1))
                    ins.then_inc(acc_full, 1)

            def attention(a, s):
                def max_bank(use):
                    at_least(pe, s.max_read, use - 1)
                    return 6

                def chunk(g, par, base, c):
                    t, h0, nh, s0, w = a.chunks[c]
                    use = base + c
                    at_least(pe, s.max_read, use - 1)
                    bank = 6 + c % 2
                    for h in range(h0, h0 + nh):
                        o = (h - h0) * w
                        diag = a.causal and s0 + w == (t + 1) * P
                        ins = nc.tensor.matmul(ps[:, bank, o:o + w], q_stack[0:ROWS, par, h, t * P:(t + 1) * P],
                                               k_stack[0:ROWS, par, h, s0:s0 + w], start=True, stop=not diag)
                        if diag:
                            ins = nc.tensor.matmul(ps[:, bank, o + w - P:o + w], identb[:, :], maskb[:, :],
                                                   start=False, stop=True)
                    ins.then_inc(s.max_full, 1)

                def turn_shift(g, base):
                    use = base + len(a.chunks)
                    pe.wait_ge(s.shift_step, 5 * (g + 1))
                    at_least(pe, s.max_read, use - 1)
                    dst = ps[:, 6 + len(a.chunks) % 2, :].bitcast(BF16)[0:PARTS * GH * TILES, 0:P]
                    nc.tensor.transpose(dst, shift[:, :, :].rearrange("p a b -> p (a b)"), identb[:, :])\
                        .then_inc(s.max_full, 1)

                def turn_out(g, base, first):
                    pe.wait_ge(s.out_copied, g + 1)
                    for q in range(2):
                        use = base + first + q
                        at_least(pe, s.max_read, use - 1)
                        for j in range(4):
                            i = 4 * q + j
                            ins = nc.tensor.transpose(ps[:, 6 + (first + q) % 2, j * P:(j + 1) * P],
                                                      out_t[:, i * P:(i + 1) * P], identf[:, :])
                        ins.then_inc(s.max_full, 1)

                def scores(g, par, ui, h):
                    pieces, width = a.steps[ui]
                    unit = a.units * g + GH * ui + h
                    at_least(pe, s.exps, unit - 1)
                    for i, q0, w, off in pieces:
                        keys = min(P, a.keys - i * P)
                        o = off
                        while o < off + w:
                            n = min(512 - o % 512, off + w - o)
                            t0 = q0 + o - off
                            ins = nc.tensor.matmul(score_region[h % 2][0:keys, o:o + n],
                                                   k_stack[:, par, h, i * P:i * P + keys],
                                                   q_stack[:, par, h, t0:t0 + n], start=True, stop=True)
                            o += n
                    ins.then_inc(s.scores, 1)

                def products(g, par, ui):
                    pieces, _ = a.steps[ui]
                    slot = (a.n_steps * par + ui) % 3
                    if a.causal:
                        pe.wait_ge(s.masked, a.masks * g + a.masks_before(ui + 1))
                    else:
                        pe.wait_ge(s.exps, a.units * g + GH * (ui + 1))
                    if ui == 0:
                        pe.wait_ge(s.v_set, g + 1)
                        at_least(pe, s.out_copied, g)
                    for n, (i, q0, w, off) in enumerate(pieces):
                        for bank in range(2):
                            lo, hi = max(q0, 512 * bank), 512 * (bank + 1)
                            if lo >= hi:
                                continue
                            for h in range(GH):
                                o = off + lo - q0
                                ins = nc.tensor.matmul(out_region[32 * h:32 * h + 32, lo:hi],
                                                       v_group[0:a.kp, par, i, h, :],
                                                       probs[0:a.kp, slot, h, o:o + hi - lo],
                                                       start=(i == 0), stop=(i == a.kt - 1 or (bank == 0 and i == 3 and a.causal)),
                                                       skip_group_check=True)
                    ins.then_inc(s.pv, 1)

                pe.wait_ge(s.q_in[0], 16 * 2 * len(QP))
                for c in range(len(a.chunks)):
                    chunk(0, 0, 0, c)
                turn_shift(0, 0)
                for g in range(NG):
                    par, nxt = g % NB, (g + 1) % NB
                    base = a.m_base(g)
                    more = g + 1 < NG
                    pe.wait_ge(s.shift_in[par], 16 * PARTS * (g // NB + 1))
                    done = 0
                    if more:
                        pe.wait_ge(s.q_in[nxt], 16 * 2 * len(QP) * ((g + 1) // NB + 1))
                    for ui in range(a.n_steps):
                        for h in range(GH):
                            scores(g, par, ui, h)
                            if more:
                                upto = a.until[GH * ui + h]
                                for c in range(done, upto):
                                    chunk(g + 1, nxt, base, c)
                                done = upto
                        if ui:
                            products(g, par, ui - 1)
                        elif g:
                            products(g - 1, (g - 1) % NB, a.n_steps - 1)
                    if more:
                        turn_shift(g + 1, base)
                    if g:
                        turn_out(g - 1, base, a.m_max if more else 0)
                products(NG - 1, (NG - 1) % NB, a.n_steps - 1)
                turn_out(NG - 1, a.m_base(NG), 0)

            pe.wait_ge(consts, 7)
            for k in range(NCH):
                turn_norm(k)
                if k:
                    qkv(k - 1)
            qkv(NCH - 1)
            context()
            pe.wait_ge(split_a, 2 * U_QC)
            pe.wait_ge(acc_read, 2 * a_at["vc", 0] + 2)
            pe.wait_ge(consts, 9)
            attention(SELF, S1)
            pe.wait_ge(S1.max_read, SELF.m_base(NG) + 2)
            pe.wait_ge(mid_in, 16)
            turn_heads(NCH)
            for n in range(NCH + 1):
                if n < NCH:
                    pe.wait_ge(tp_read, 2 * t_at["o", NCH + n] + 2)
                    rows_product(("w", NCH + n), lambda k, j: ho_t[:, k, j * P:(j + 1) * P],
                                 lambda k: wmid[:, k, W1:W1 + C], KC)
                if n + 1 < NCH:
                    turn_heads(NCH + n + 1)
                if n:
                    k = NCH + n - 1
                    turn_norm(k)
                    pe.wait_ge(tp_read, 2 * t_at["x", k] + 2)
                    for hh in range(2):
                        project(U_QC + 2 * (n - 1) + hh, k,
                                lambda kc: wmid[:, kc, WQ_C + hh * P:WQ_C + (hh + 1) * P],
                                lambda kc: xn_t[:, k % 2, kc, :], CHUNK)
            pe.wait_ge(split_a, 2 * U_H)
            attention(CROSS, S2)
            pe.wait_ge(S2.max_read, CROSS.m_base(NG) + 2)
            pe.wait_ge(ff_in, 32)

            def feed_out(n):
                pe.wait_ge(hid_done, (FF // P) * (n + 1))
                rows_product(("f", n), lambda k, j: hid_t[:, k, j * P:(j + 1) * P], lambda k: wf2[:, k, :], FF // P)

            turn_heads(2 * NCH)
            for n in range(NCH):
                k = 2 * NCH + n
                pe.wait_ge(tp_read, 2 * t_at["o", k] + 2)
                rows_product(("w", k), lambda kk, j: ho_t[:, kk, j * P:(j + 1) * P],
                             lambda kk: wmid[:, kk, W2:W2 + C], KC)
                if n + 1 < NCH:
                    turn_heads(k + 1)
                if n:
                    feed_out(n - 1)
                turn_norm(k)
                pe.wait_ge(tp_read, 2 * t_at["x", k] + 2)
                for f in range(FF // P):
                    project(U_H + n * (FF // P) + f, k, lambda kc: wf1[:, kc, f * P:(f + 1) * P],
                            lambda kc: xn_t[:, k % 2, kc, :], CHUNK)
            feed_out(NCH - 1)

        @block.vector
        def _(dve):
            def ln_sums(k):
                n, p = k % NCH, k % 2
                at_least(dve, ln_var, k)
                at_least(dve, ln_done, CT * (k - 1))
                for j in range(CT):
                    nc.vector.bn_stats(stats[:, j, :], xs[:, n * CT + j, :]).then_inc(ln_stats, 1)
                dve.wait_ge(ln_stats, CT * (k + 1))
                for j in range(CT):
                    ins = nc.vector.bn_aggr(mean_var[:, p, j, :], stats[:, j, :])
                ins.then_inc(ln_var, 1)

            def ln_apply(k):
                n, p = k % NCH, k % 2
                dve.wait_ge(ln_rstd, k + 1)
                if 2 <= k < NCH or NCH + 2 <= k < 2 * NCH or 2 * NCH + 2 <= k:
                    dve.wait_ge(tp_full, 2 * t_at["x", k - 2] + 2)
                for j in range(CT):
                    nc.vector.tensor_scalar(xn[:, p, j, :], xs[:, n * CT + j, :], mean_var[:, p, j, 0:1],
                                            rstd[:, p, j:j + 1], ALU.subtract, ALU.mult).then_inc(ln_done, 1)

            def split(u):
                width, _, _ = split_unit(u)
                p, f = parts[:, u % 4, :, 0:width], full[:, u % 2, 0:width]
                r = rest[:, u % 2, 0:width]
                dve.wait_ge(split_a, 2 * u + 2)
                nc.vector.tensor_tensor(r, f, p[:, 0, :], ALU.subtract).then_inc(split_v, 1)
                dve.wait_ge(split_v, 3 * u + 1)
                nc.vector.tensor_copy(p[:, 1, :], r).then_inc(split_v, 1)
                dve.wait_ge(split_v, 3 * u + 2)
                nc.vector.tensor_tensor(p[:, 2, :], r, p[:, 1, :], ALU.subtract).then_inc(split_v, 1)

            def add_v(n):
                b, i0 = n // 2, (n % 2) * CT
                for half in range(2):
                    dve.wait_ge(acc_full, 2 * a_at["v", n] + half + 1)
                    for j in (2 * half, 2 * half + 1):
                        dst = v_self[:, 4 * b:4 * b + 4, i0 + j, :]
                        ins = nc.vector.tensor_tensor(dst, acc[:, j, :].rearrange("p (g c) -> p g c", g=4),
                                                      row[:, BV_S, :].rearrange("p (g c) -> p g c", g=4), ALU.add)
                    ins.then_inc(acc_read, 1)

            def add_rows(key, n, bias_k):
                i = a_at[key]
                dve.wait_ge(bias_added, bias_k + 1)
                for half in range(2):
                    dve.wait_ge(acc_full, 2 * i + half + 1)
                    t0 = n * CT + 2 * half
                    xt = xs[:, t0:t0 + 2, :]
                    nc.vector.tensor_tensor(xt, acc[:, 2 * half:2 * half + 2, :], xt, ALU.add)\
                        .then_inc(acc_read, 1)
                dve.wait_ge(acc_read, 2 * i + 2)

            def attention(a, s):
                def reduce(use, c):
                    t, h0, nh, s0, w = a.chunks[c]
                    dve.wait_ge(s.max_full, use + 1)
                    dst = max_b[:, h0:h0 + nh, t - 4:t - 3] if s0 else max_a[:, h0:h0 + nh, t:t + 1]
                    nc.vector.tensor_reduce(dst, ps[:, 6 + c % 2, 0:nh * w].rearrange("p (h w) -> p h w", h=nh),
                                            AX.X, ALU.max).then_inc(s.max_read, 1)

                def maxima(g, base):
                    for c in range(len(a.chunks)):
                        reduce(base + c, c)
                    dve.wait_ge(s.max_read, base + len(a.chunks))
                    nc.vector.tensor_tensor(max_a[:, :, 4:8], max_a[:, :, 4:8],
                                            max_b[:, :, :] if a.causal else max_a[:, :, 4:8], ALU.max)\
                        .then_inc(s.maxima, 1)

                def copy_shift(g, base):
                    dve.wait_ge(s.max_full, base + len(a.chunks) + 1)
                    if g:
                        dve.wait_ge(s.shift_in[(g - 1) % NB], 16 * PARTS * ((g - 1) // NB + 1))
                    src = ps[:, 6 + len(a.chunks) % 2, :].bitcast(BF16)[0:PARTS * GH * TILES, 0:P]
                    nc.vector.tensor_copy(shift_t[:, :], src).then_inc(s.max_read, 1)

                def norm_out(g, base, first):
                    for q in range(2):
                        bank = ps[:, 6 + (first + q) % 2, :].rearrange("p (u c) -> p u c", c=32)
                        dve.wait_ge(s.max_full, base + first + q + 1)
                        nc.vector.reciprocal(recip[:, q, :], bank[:, :, D]).then_inc(s.recips, 1)
                        dve.wait_ge(s.recips, 2 * g + q + 1)
                        dst = heads_out[:, g // 2, 4 * q:4 * q + 4, g % 2 * GW:g % 2 * GW + GW]
                        nc.vector.tensor_tensor(dst.rearrange("p i (h d) -> p i h d", d=D),
                                                bank[:, :, 0:D].rearrange("p (i h) d -> p i h d", h=GH),
                                                recip[:, q, :].rearrange("p (i h o) -> p i h o", h=GH, o=1)
                                                .to_broadcast([P, 4, GH, D]), ALU.mult).then_inc(s.max_read, 1)

                maxima(0, 0)
                copy_shift(0, 0)
                for g in range(NG):
                    base = a.m_base(g)
                    more = g + 1 < NG
                    if more:
                        maxima(g + 1, base)
                        copy_shift(g + 1, base)
                    if g:
                        norm_out(g - 1, base, a.m_max if more else 0)
                norm_out(NG - 1, a.m_base(NG), 0)

            dve.wait_ge(x_in[0], 16)
            ln_sums(0)
            for n in range(NCH):
                if n + 1 < NCH:
                    dve.wait_ge(x_in[n + 1], 16)
                    ln_sums(n + 1)
                ln_apply(n)
                if n == 0:
                    dve.wait_ge(row_in, 16)
                if n:
                    for u in range(4):
                        split(4 * (n - 1) + u)
                    add_v(n - 1)
            for u in range(4):
                split(4 * (NCH - 1) + u)
            add_v(NCH - 1)
            for u in range(2):
                split(U_KC + u)
            for b in range(B):
                dve.wait_ge(acc_full, 2 * a_at["vc", 0] + b + 1)
                nc.vector.tensor_tensor(v_ctx[:, 4 * b:4 * b + 4, :],
                                        acc[0:S_CTX, 2 * b, :].rearrange("p (g c) -> p g c", g=4),
                                        row[0:S_CTX, BV_C, :].rearrange("p (g c) -> p g c", g=4), ALU.add)\
                    .then_inc(acc_read, 1)
            attention(SELF, S1)
            dve.wait_ge(S1.pv, SELF.n_steps * NG)
            for n in range(NCH + 2):
                if n < NCH:
                    add_rows(("w", NCH + n), n, n)
                    ln_sums(NCH + n)
                if n >= 2:
                    for u in range(2):
                        split(U_QC + 2 * (n - 2) + u)
                if n < NCH:
                    ln_apply(NCH + n)
            attention(CROSS, S2)
            dve.wait_ge(S2.pv, CROSS.n_steps * NG)
            for n in range(NCH):
                add_rows(("w", 2 * NCH + n), n, NCH + n)
                ln_sums(2 * NCH + n)
                ln_apply(2 * NCH + n)
                if n:
                    add_rows(("f", n - 1), n - 1, 2 * NCH + n - 1)
            add_rows(("f", NCH - 1), NCH - 1, 3 * NCH - 1)


def kernel(x, ctx_1024, **w):
    import numpy as np
    import concourse.bacc as bacc
    from concourse.bass_utils import run_bass_kernel_spmd as run

    w = {k.removeprefix("L0_xattn_"): np.asarray(v) for k, v in w.items()}

    def flat(name):
        return w[name].transpose(1, 0, 2).reshape(C, H * D)

    def channel_cols(v):
        return v.reshape(-1, P).T

    arrays = {
        "x": np.asarray(x),
        "w_qkv": np.concatenate([flat("Wq_s"), flat("Wk_s"), flat("Wv_s")], 1),
        "w_ctx": np.concatenate([flat("Wk_c"), flat("Wv_c")], 1),
        "w_mid": np.concatenate([w["W1"], flat("Wq_c"), w["W2"]], 1),
        "w_f1": w["Wf1"],
        "w_f2": w["Wf2"],
        "ctx_t": np.asarray(ctx_1024).reshape(B * S_CTX, C).T,
        "cols": np.concatenate([channel_cols(w[k]) for k in
                                ("bq_s", "bk_s", "bq_c", "bk_c", "g1", "be1", "g2", "be2", "g3", "be3", "bf1")], 1),
        "rows": np.stack([w[k].reshape(C) for k in ("bv_s", "b1", "bv_c", "b2", "bf2")]),
    }
    arrays = {k: np.ascontiguousarray(v) for k, v in arrays.items()}
    nc = bacc.Bacc("TRN2", target_bir_lowering=False, num_devices=1)
    args = [nc.dram_tensor(f"in_{k}", v.shape, mybir.dt.from_np(v.dtype), kind="ExternalInput").ap()
            for k, v in arrays.items()]
    out = nc.dram_tensor("out", (B, T, C), F32, kind="ExternalOutput").ap()
    build(nc, *args, out)
    r = run(nc, [{f"in_{k}": v for k, v in arrays.items()}], core_ids=[0])
    return r.results[0]["out"]
```

```python
from contextlib import ExitStack

import concourse.bass as bass
from concourse import mybir

ALU = mybir.AluOpType
ACT = mybir.ActivationFunctionType
AX = mybir.AxisListType
F32 = mybir.dt.float32
F32R = mybir.dt.float32r
BF16 = mybir.dt.bfloat16

P = 128
B, T, C, H, D = 2, 1024, 256, 16, 16
S_CTX = 77
FF = 4 * C
EPS = 1e-5
HI, LO = 0, 1
PASSES = [(HI, HI), (HI, LO), (LO, HI)]
KC = C // P
CHUNK = 512
CT = CHUNK // P
NCH = B * T // CHUNK
TILES = T // P
GH = 4
NG = B * H // GH
GW = GH * D
PARTS = 3
QP = [0, 0, 0, 1, 1, 2]
KP = [0, 1, 2, 0, 1, 0]
ROWS = D * len(QP)
ROWS_S = ROWS + PARTS
SCALE = float(D) ** 0.5
NEG = -1e30
BANK = 512
M_BANKS = 3
S_BANKS = 3
P_SLOTS = 3

BQ_S, BK_S, BQ_C, BK_C, G1, BE1, G2, BE2, G3, BE3, BF1 = 0, 2, 4, 6, 8, 10, 12, 14, 16, 18, 20
NCOLS = 20 + FF // P
BV_S, B1, BV_C, B2, BF2 = range(5)
W1, WQ_C, W2 = 0, C, 2 * C


class Attention:

    def __init__(self, causal, keys, buffers, lead, gap):
        self.causal, self.keys, self.nb = causal, keys, buffers
        self.kt = -(-keys // P)
        self.kp = min(P, keys)
        self.steps = []
        for tiles in ([[0], [1], [2], [3], [4, 5], [6, 7]] if causal else [[0]]):
            off, pieces = 0, []
            for i in tiles:
                w = T - i * P if causal else T
                pieces.append((i, T - w, w, off))
                off += w
            self.steps.append((pieces, off))
        self.n_steps = len(self.steps)
        self.units = [(ui, h, k) for ui, (_, width) in enumerate(self.steps)
                      for h in range(GH) for k in range(-(-width // BANK))]
        self.chunks = []
        for t in range(TILES):
            keys_t = (t + 1) * P if causal else keys
            for s in range(0, keys_t, BANK):
                w = min(BANK, keys_t - s)
                nh = min(BANK // w, GH)
                self.chunks += [(t, h, nh, s, w) for h in range(0, GH, nh)]
        self.order(lead, gap)

    def order(self, lead, gap):
        def spread(costs):
            total, at, out = sum(costs), 0.0, []
            for c in costs:
                out.append(at / total)
                at += c
            return out
        unit_at = spread([self.unit_width(u) + BANK for u in range(len(self.units))])
        chunk_at = spread([nh * w + 64 for _, _, nh, _, w in self.chunks])
        stream = [(g + chunk_at[c], ("chunk", g, c)) for g in range(NG) for c in range(len(self.chunks))]
        stream += [(g + 1 + gap, ("shift", g)) for g in range(NG)]
        stream.sort(key=lambda e: e[0])
        self.pe, self.uses = [], []

        def use(what):
            self.pe.append(("m", len(self.uses)))
            self.uses.append(what)

        def outputs(g):
            if g >= 0:
                use(("out", g, 0))
                use(("out", g, 1))
        for g in range(NG):
            for u, (ui, h, k) in enumerate(self.units):
                while stream and stream[0][0] <= g + unit_at[u] + lead:
                    use(stream.pop(0)[1])
                self.pe.append(("score", g, u))
                if u + 1 == len(self.units) or self.units[u + 1][0] != ui:
                    if ui:
                        self.pe.append(("product", g, ui - 1))
                    elif g:
                        self.pe.append(("product", g - 1, self.n_steps - 1))
                    if ui == 1 or self.n_steps == 1:
                        outputs(g - 1 if ui else g - 2)
        if self.n_steps == 1:
            outputs(NG - 2)
        self.pe.append(("product", NG - 1, self.n_steps - 1))
        outputs(NG - 1)
        self.use_at = {what: i for i, what in enumerate(self.uses)}

    def unit_width(self, u):
        ui, _, k = self.units[u]
        return min(BANK, self.steps[ui][1] - k * BANK)

    def unit_index(self, g, ui):
        return g * len(self.units) + sum(u[0] < ui for u in self.units)

    def step_end(self, g, u):
        ui = self.units[u][0]
        return ui if u + 1 == len(self.units) or self.units[u + 1][0] != ui else None

    def masks(self, g, ui):
        return self.kt * g + sum(len(pieces) for pieces, _ in self.steps[:ui + 1])

    def probs_slot(self, g, ui):
        return (self.n_steps * g + ui) % P_SLOTS


SELF = Attention(True, T, buffers=3, lead=1.35, gap=0.12)
CROSS = Attention(False, S_CTX, buffers=5, lead=2.3, gap=0.5)
SELF_EARLY = [14, 18, 22, 26, 30, 36, 44]
CROSS_EARLY = [12, 16]


def at_least(eng, sem, value):
    if not isinstance(value, int) or value > 0:
        eng.wait_ge(sem, value)


def build(nc, x, w_qkv, w_ctx, w_mid, w_f1, w_f2, ctx_t, cols, rows, out):
    x_d = x.rearrange("b t c -> (b t) c").rearrange("(n p) c -> p n c", p=P)
    out_d = out.rearrange("b t c -> (b t) c").rearrange("(n p) c -> p n c", p=P)
    q_dram = nc.dram_tensor("q_parts", (PARTS, NG, GW, T), BF16).ap()
    k_dram = nc.dram_tensor("k_parts", (PARTS, NG, GW, T), BF16).ap()
    qc_dram = nc.dram_tensor("qc_parts", (PARTS, NG, GW, T), BF16).ap()
    kc_dram = nc.dram_tensor("kc_parts", (PARTS, NG, GW, S_CTX), BF16).ap()

    with ExitStack() as ctx:
        def sb(name, shape, dt=F32):
            return ctx.enter_context(nc.sbuf_tensor(name, shape, dt))

        def sem(name):
            return ctx.enter_context(nc.semaphore(name))

        xs = sb("xs", [P, NCH * CT, C])
        wmid = sb("wmid", [P, KC, 3 * C])
        col = sb("col", [P, NCOLS])
        row = sb("row", [P, 5, C])
        identf = sb("identf", [P, P])
        identb = sb("identb", [P, P], BF16)
        maskb = sb("maskb", [P, P], BF16)
        neghalf = sb("neghalf", [P, CT])
        arena_h = sb("arena_h", [P, NG // 2 * TILES * 2 * GW])
        heads_out = arena_h[:, :].rearrange("p (g i c) -> p g i c", g=NG // 2, i=TILES)
        n_qkv, n_ctx = KC * 3 * C, KC * 2 * C
        wqkv = arena_h[:, 0:n_qkv].rearrange("p (k n) -> p k n", k=KC)
        wctx = arena_h[:, n_qkv:n_qkv + n_ctx].rearrange("p (k n) -> p k n", k=KC)
        ctxt = arena_h[:, n_qkv + n_ctx:n_qkv + n_ctx + KC * B * S_CTX].rearrange("p (k n) -> p k n", k=KC)
        arena_v = sb("arena_v", [P, NG * TILES * GW])
        v_self = arena_v[:, :].rearrange("p (g i c) -> p g i c", g=NG, i=TILES)
        wf1 = arena_v[:, 0:KC * FF].rearrange("p (k n) -> p k n", k=KC)
        wf2 = arena_v[:, KC * FF:2 * KC * FF].rearrange("p (k n) -> p k n", k=FF // P)
        v_ctx = sb("v_ctx", [S_CTX, NG, GW])
        wf1r = sb("wf1r", [P, 2, KC, FF], F32R)
        v_group = sb("v_group", [P, 3, TILES, GH, 32])
        out_t = sb("out_t", [P, T])
        max_a = sb("max_a", [P, 2, GH, TILES])
        max_b = sb("max_b", [P, 2, GH, 4])
        neg_m = sb("neg_m", [P, GH * TILES])
        neg_r = sb("neg_r", [P, GH * TILES])
        shift = sb("shift", [P, PARTS, GH * TILES], BF16)
        shift_t = sb("shift_t", [PARTS * GH * TILES, P], BF16)
        recip = sb("recip", [P, 2, 16])
        parts = sb("parts", [P, 4, PARTS, CHUNK], BF16)
        stats = sb("stats", [P, CT, 6])
        mean_var = sb("mean_var", [P, 2, CT, 2])
        veps = sb("veps", [P, 2, CT])
        rstd = sb("rstd", [P, 2, CT])
        with ExitStack() as attention_only:
            stacks = attention_only.enter_context(nc.sbuf_tensor("stacks", [ROWS_S, 6, GH, T], BF16))
            arena_p = attention_only.enter_context(nc.sbuf_tensor("arena_p", [P, P_SLOTS * GH * T], F32))
        q_stack = stacks[:, 0:5, :, :]
        k_self = stacks[:, 3:6, :, :]
        k_ctx = stacks[:, 5, :, :].rearrange("p h t -> p (h t)")[:, 0:NG * GH * S_CTX]\
            .rearrange("p (g h t) -> p g h t", g=NG, h=GH)
        probs = arena_p[:, :].rearrange("p (s h t) -> p s h t", s=P_SLOTS, h=GH)
        wf2r = sb("wf2r", [P, 2, FF // P, C], F32R)
        hid_r = sb("hid_r", [P, 2, FF // P, CHUNK], F32R)
        xn_r = sb("xn_r", [P, 2, 2, KC, CHUNK], F32R)
        at = [4 * 1024]

        def scratch(*shape):
            n = 1
            for s in shape:
                n *= s
            a = arena_p[:, at[0]:at[0] + n]
            at[0] += n
            names = "abcd"[:len(shape)]
            if len(shape) == 1:
                return a
            return a.rearrange("p (" + " ".join(names) + ") -> p " + " ".join(names),
                               **{k: s for k, s in zip(names, shape)})
        xn = scratch(2, CT, C)
        xn_t = scratch(2, KC, CHUNK)
        full = scratch(2, CHUNK)
        rest = scratch(2, CHUNK)
        ho_t = out_t[:, :].rearrange("p (k t) -> p k t", k=KC)

        ps = ctx.enter_context(nc.psum_tensor("ps", [P, 8, 512], F32))
        acc = ps[:, 6:8, :].rearrange("p b (j c) -> p (b j) c", c=C)
        out_region = ps[:, 6:8, :].rearrange("p b n -> p (b n)")

        def m_bank(use):
            return ps[:, S_BANKS + use % M_BANKS, :]

        x_in = [sem(f"x_in{n}") for n in range(NCH)]
        wqkv_in, col_in, row_in, ctx_in, mid_in, ff_in = (sem(n) for n in
            ("wqkv_in", "col_in", "row_in", "ctx_in", "mid_in", "ff_in"))
        consts = sem("consts")
        ln_stats, ln_var, ln_veps, ln_rstd, ln_done = (sem(n) for n in
            ("ln_stats", "ln_var", "ln_veps", "ln_rstd", "ln_done"))
        bias_added = sem("bias_added")
        tp_full, tp_read = sem("tp_full"), sem("tp_read")
        ring_full = sem("ring_full")
        acc_full, acc_read = sem("acc_full"), sem("acc_read")
        split_a, split_v = sem("split_a"), sem("split_v")
        parts_out = [sem(f"parts_out{s}") for s in range(4)]
        wf1_halves, wf2_halves = sem("wf1_halves"), sem("wf2_halves")
        xn_full, xn_low = sem("xn_full"), sem("xn_low")
        hid_full, hid_done, hid_low = sem("hid_full"), sem("hid_done"), sem("hid_low")
        out_done = sem("out_done")

        class Sems:
            def __init__(self, pre, a):
                s = lambda name: sem(f"{pre}_{name}")
                self.q_in = [s(f"q_in{p}") for p in range(a.nb)]
                self.k_in = s("k_in")
                self.shift_in = [s(f"shift_in{p}") for p in range(a.nb)]
                self.v_set = s("v_set")
                self.max_full, self.max_read = s("max_full"), s("max_read")
                self.maxima = s("maxima")
                self.shift_step = s("shift_step")
                self.scores, self.exps = s("scores"), s("exps")
                self.masked = s("masked")
                self.pv = s("pv")
                self.out_copied = s("out_copied")
                self.recips = s("recips")
        S1, S2 = Sems("self", SELF), Sems("cross", CROSS)

        t_order = [("x", k) for k in range(NCH)]
        t_order.append(("o", NCH))
        for n in range(NCH + 1):
            if n + 1 < NCH:
                t_order.append(("o", NCH + n + 1))
            if n:
                t_order.append(("x", NCH + n - 1))
        t_order += [(kind, 2 * NCH + n) for kind, n in
                    [("o", 0), ("o", 1)] + [e for n in range(NCH) for e in (("x", n), ("o", n + 2)) if e[1] < NCH]]
        t_at = {key: i for i, key in enumerate(t_order)}
        a_order = [("v", n) for n in range(NCH)] + [("vc", 0)] + [("w", NCH + n) for n in range(NCH)]
        a_order += [("w", 2 * NCH), ("w", 2 * NCH + 1)]
        for n in range(NCH):
            a_order.append(("f", n))
            if n + 2 < NCH:
                a_order.append(("w", 2 * NCH + n + 2))
        a_at = {key: i for i, key in enumerate(a_order)}
        U_KC, U_QC, U_H = 4 * NCH, 4 * NCH + 2, 4 * NCH + 2 + 2 * NCH

        def split_unit(u):
            if u < U_KC:
                n, s = divmod(u, 4)
                dst, c0 = (q_dram, BQ_S) if s < 2 else (k_dram, BK_S)
                hh = s % 2
            elif u < U_QC:
                hh = u - U_KC
                d = [kc_dram[:, 4 * b + 2 * hh:4 * b + 2 * hh + 2, :, :] for b in range(B)]
                return B * S_CTX, BK_C + hh, [(a.rearrange("p g r t -> (g r) p t"), b * S_CTX, S_CTX)
                                              for b, a in enumerate(d)]
            else:
                n, hh = divmod(u - U_QC, 2)
                dst, c0 = qc_dram, BQ_C
            b, t0 = n // 2, (n % 2) * CHUNK
            a = dst[:, 4 * b + 2 * hh:4 * b + 2 * hh + 2, :, t0:t0 + CHUNK]
            return CHUNK, c0 + hh, [(a.rearrange("p g r t -> (g r) p t"), 0, CHUNK)]

        def parts_landed(u):
            return 16 * sum(2 if U_KC <= v < U_QC else 1 for v in range(u % 4, u + 1, 4))

        def unit_bank(u):
            if u < U_KC:
                return (2, 6, 7, 2)[u % 4]
            return (2, 6)[u % 2] if u < U_H else 2 + u % 4

        block = ctx.enter_context(nc.Block())

        @block.sync
        def _(sp):
            sp.dma_start(xs[:, 0:CT, :], x_d[:, 0:CT, :]).then_inc(x_in[0], 16)
            sp.dma_start(col[:, :], cols).then_inc(col_in, 16)
            sp.dma_start(wqkv[:, :, :], w_qkv.rearrange("(k p) n -> p k n", p=P)).then_inc(wqkv_in, 16)
            for n in range(1, NCH):
                sp.dma_start(xs[:, n * CT:(n + 1) * CT, :], x_d[:, n * CT:(n + 1) * CT, :]).then_inc(x_in[n], 16)
                if n == 1:
                    sp.dma_start(row[:, :, :], rows.rearrange("(o r) c -> o r c", o=1).to_broadcast([P, 5, C]))\
                        .then_inc(row_in, 16)
            sp.dma_start(wctx[:, :, :], w_ctx.rearrange("(k p) n -> p k n", p=P)).then_inc(ctx_in, 16)
            sp.dma_start(ctxt[:, :, :], ctx_t.rearrange("(k p) n -> p k n", p=P)).then_inc(ctx_in, 16)
            sp.dma_start(wmid[:, :, :], w_mid.rearrange("(k p) n -> p k n", p=P)).then_inc(mid_in, 16)

            def store_parts(u):
                width, _, dsts = split_unit(u)
                sp.wait_ge(split_v, 3 * u + 3)
                for dst, c0, w in dsts:
                    sp.dma_start(dst, parts[:, u % 4, :, c0:c0 + w]).then_inc(parts_out[u % 4], 16)

            def load_blocks(src, dst, which, gs, arrived):
                for blk in range(len(QP)):
                    sp.dma_start(dst[blk * D:(blk + 1) * D],
                                 src[which[blk], gs, :, :].rearrange("g (h d) t -> d (g h) t", d=D))\
                        .then_inc(arrived, 16)

            def load_stacks(a, s, g):
                par = g % a.nb
                at_least(sp, s.scores, len(a.units) * (g - a.nb + 1))
                load_blocks(q_dram if a.causal else qc_dram, q_stack[:, par, :, :], QP, slice(g, g + 1), s.q_in[par])
                if a.causal:
                    load_blocks(k_dram, k_self[:, par, :, :], KP, slice(g, g + 1), s.q_in[par])

            def attention(a, s, lo, hi=None):
                def load_shift(g):
                    sp.wait_ge(s.max_read, a.use_at["shift", g] + 1)
                    for k in range(PARTS):
                        n = GH * TILES
                        dst = q_stack[ROWS + k:ROWS + k + 1, g % a.nb, :, :]
                        sp.dma_start(dst.rearrange("o h (i t) -> o (h i) t", t=P), shift_t[k * n:(k + 1) * n, :])\
                            .then_inc(s.shift_in[g % a.nb], 16)

                for op, *what in a.pe[lo:hi]:
                    if op == "m" and a.uses[what[0]][0] == "shift":
                        load_shift(a.uses[what[0]][1])
                    if op == "score" and what[1] + 1 == len(a.units):
                        if what[0] + a.nb < NG:
                            load_stacks(a, s, what[0] + a.nb)
                        if a.causal and what[0] == NG - 3:
                            sp.wait_ge(S1.scores, len(a.units) * (NG - 2))
                            load_blocks(kc_dram, k_ctx.rearrange("p g h t -> p (g h) t"), KP, slice(0, NG), S2.k_in)

            def wait_parts(units):
                for slot in range(4):
                    sp.wait_ge(parts_out[slot], parts_landed(max(u for u in range(units) if u % 4 == slot)))

            for u in range(U_QC):
                if u == 2 * NCH:
                    wait_parts(2 * NCH)
                    load_stacks(SELF, S1, 0)
                if u == 3 * NCH:
                    load_stacks(SELF, S1, 1)
                store_parts(u)
            load_stacks(SELF, S1, 2)
            wait_parts(U_QC)
            attention(SELF, S1, 0)
            sp.wait_ge(S1.v_set, NG)
            sp.dma_start(wf1, w_f1.rearrange("(k p) n -> p k n", p=P)).then_inc(ff_in, 16)
            sp.dma_start(wf2, w_f2.rearrange("(k p) n -> p k n", p=P)).then_inc(ff_in, 16)
            for n in range(NCH):
                if n == NCH - 1:
                    attention(CROSS, S2, 0, CROSS_EARLY[-1])
                store_parts(U_QC + 2 * n)
                store_parts(U_QC + 2 * n + 1)
                if n == 1:
                    wait_parts(U_QC + NCH)
                if n >= 1 and n < NCH - 1:
                    load_stacks(CROSS, S2, 2 * n - 2)
                    load_stacks(CROSS, S2, 2 * n - 1)
            wait_parts(U_H)
            load_stacks(CROSS, S2, 4)
            attention(CROSS, S2, CROSS_EARLY[-1])
            for n in range(NCH):
                for half in range(2):
                    sp.wait_ge(acc_read, 2 * a_at["f", n] + half + 1)
                    t0 = n * CT + 2 * half
                    sp.dma_start(out_d[:, t0:t0 + 2, :], xs[:, t0:t0 + 2, :]).then_inc(out_done, 16)
            sp.wait_ge(out_done, 16 * 2 * NCH)

        @block.gpsimd
        def _(pool):
            c = [0]

            def made(ins, n=1):
                ins.then_inc(consts, 1)
                c[0] += 1
            made(pool.memset(identf[:, :], 0.0))
            made(pool.memset(identb[:, :], 0.0))
            made(pool.memset(maskb[:, :], 0.0))
            made(pool.memset(neghalf[:, :], -0.5))
            pool.wait_ge(consts, 4)
            for m in (identf, identb):
                made(pool.affine_select(out=m[:, :], in_=m[:, :], compare_op=ALU.not_equal, fill=1.0, base=0,
                                        pattern=[[-1, P]], channel_multiplier=1))
            made(pool.affine_select(out=maskb[:, :], in_=maskb[:, :], compare_op=ALU.is_ge, fill=NEG, base=0,
                                    pattern=[[-1, P]], channel_multiplier=1))

            def ln_root(k):
                pool.wait_ge(ln_var, k + 1)
                pool.tensor_scalar(veps[:, k % 2, :], mean_var[:, k % 2, :, 1], EPS, None, ALU.add)\
                    .then_inc(ln_veps, 1)
                pool.wait_ge(ln_veps, k + 1)
                pool.tensor_tensor(rstd[:, k % 2, :], veps[:, k % 2, :], neghalf[:, :], ALU.pow)\
                    .then_inc(ln_rstd, 1)

            def add_bias(k):
                n = k % NCH
                r = (B1, B2, BF2)[k // NCH]
                pool.wait_ge(ln_done, CT * (k + 1))
                if k == 0:
                    pool.wait_ge(row_in, 16)
                for j in range(CT):
                    xt = xs[:, n * CT + j, :]
                    ins = pool.tensor_tensor(xt, xt, row[:, r, :], ALU.add)
                ins.then_inc(bias_added, 1)

            def weight_halves(halves, w, done):
                pool.tensor_copy(halves[:, HI], w).then_inc(done, 1)
                pool.wait_ge(done, 1)
                pool.tensor_tensor(halves[:, LO], w, halves[:, HI], ALU.subtract).then_inc(done, 1)

            def attention(a, s):
                def set_v(g):
                    pool.wait_ge(acc_read, 2 * a_at["v", 1 + 2 * (g // (NG // B))] + 2 if a.causal
                                 else 2 * a_at["vc", 0] + 2)
                    if a.causal:
                        at_least(pool, s.pv, a.n_steps * (g - 2))
                        src = v_self[:, g, :, :].rearrange("p i (h d) -> p i h d", d=D)
                        dst = v_group[:, g % 3, :, :, 0:D]
                    else:
                        src = v_ctx[:, :, :].rearrange("p g (h d) -> p g h d", d=D)
                        dst = v_group[0:S_CTX, 0, :, :, 0:D]
                    pool.tensor_copy(dst, src).then_inc(s.v_set, 1)

                def split_shift(g):
                    pool.wait_ge(s.maxima, g + 1)
                    m = max_a[:, g % 2, :, :].rearrange("p h i -> p (h i)")
                    base = 5 * g
                    pool.tensor_scalar(neg_m[:, :], m, -1.0, None, ALU.mult).then_inc(s.shift_step, 1)
                    pool.wait_ge(s.shift_step, base + 1)
                    pool.tensor_copy(shift[:, 0, :], neg_m[:, :]).then_inc(s.shift_step, 1)
                    pool.wait_ge(s.shift_step, base + 2)
                    pool.tensor_tensor(neg_r[:, :], neg_m[:, :], shift[:, 0, :], ALU.subtract)\
                        .then_inc(s.shift_step, 1)
                    pool.wait_ge(s.shift_step, base + 3)
                    pool.tensor_copy(shift[:, 1, :], neg_r[:, :]).then_inc(s.shift_step, 1)
                    pool.wait_ge(s.shift_step, base + 4)
                    pool.tensor_tensor(shift[:, 2, :], neg_r[:, :], shift[:, 1, :], ALU.subtract)\
                        .then_inc(s.shift_step, 1)

                def mask(g, ui):
                    pool.wait_ge(s.exps, a.unit_index(g, ui + 1))
                    for i, q0, w, off in a.steps[ui][0]:
                        blk = probs[:, a.probs_slot(g, ui), :, off:off + P]
                        pool.affine_select(out=blk, in_=blk, compare_op=ALU.is_ge, fill=0.0, base=0,
                                           pattern=[[0, GH], [1, P]], channel_multiplier=-1).then_inc(s.masked, 1)

                set_v(0)
                for op, *what in a.pe:
                    if op == "m" and a.uses[what[0]] == ("chunk", a.uses[what[0]][1], len(a.chunks) - 1):
                        split_shift(a.uses[what[0]][1])
                    if op == "score" and a.causal and a.step_end(*what) is not None:
                        mask(what[0], a.step_end(*what))
                        if a.step_end(*what) == 0 and what[0] + 1 < NG:
                            set_v(what[0] + 1)

            made(pool.memset(v_group[:, :, :, :, D:32], 1.0))
            ln_root(0)
            for k in range(1, NCH):
                ln_root(k)
                add_bias(k - 1)
            add_bias(NCH - 1)
            pool.wait_ge(bias_added, NCH)
            made(pool.memset(k_self[ROWS:ROWS_S, :, :, :], 1.0))
            pool.wait_ge(consts, 9)
            attention(SELF, S1)
            for k in range(NCH, 2 * NCH):
                ln_root(k)
                add_bias(k)
            attention(CROSS, S2)
            pool.wait_ge(ff_in, 32)
            weight_halves(wf1r, wf1, wf1_halves)
            ln_root(2 * NCH)
            ln_root(2 * NCH + 1)
            pool.wait_ge(S2.pv, CROSS.n_steps * NG)
            weight_halves(wf2r, wf2, wf2_halves)
            add_bias(2 * NCH)
            add_bias(2 * NCH + 1)
            for k in range(2 * NCH + 2, 3 * NCH):
                ln_root(k)
                add_bias(k)

        @block.scalar
        def _(act):
            def copy_norm(k):
                i, p = t_at["x", k], k % 2
                gcol, bcol = ((G1, BE1), (G2, BE2), (G3, BE3))[k // NCH]
                for kc in range(KC):
                    act.wait_ge(tp_full, 2 * i + kc + 1)
                    if kc == 0 and 2 <= k < NCH:
                        act.wait_ge(acc_full, 2 * a_at["v", k - 2] + 2)
                    if kc == 0 and NCH + 2 <= k < 2 * NCH:
                        act.wait_ge(ring_full, U_QC + 2 * (k - NCH - 2) + 2)
                    if kc == 0 and 2 * NCH + 2 <= k:
                        act.wait_ge(ring_full, U_H + 8 * (k - 2 * NCH - 2) + 8)
                        act.wait_ge(xn_low, KC * (k - 2 * NCH - 1))
                    if k >= 2 * NCH:
                        nc.scalar.activation(xn_r[:, HI, p, kc, :], ps[:, kc, :], ACT.Identity,
                                             scale=col[:, gcol + kc:gcol + kc + 1],
                                             bias=col[:, bcol + kc:bcol + kc + 1]).then_inc(xn_full, 1)
                    nc.scalar.activation(xn_t[:, p, kc, :], ps[:, kc, :], ACT.Identity,
                                         scale=col[:, gcol + kc:gcol + kc + 1],
                                         bias=col[:, bcol + kc:bcol + kc + 1]).then_inc(tp_read, 1)

            def copy_heads(k):
                i = t_at["o", k]
                for kc in range(KC):
                    act.wait_ge(tp_full, 2 * i + kc + 1)
                    if kc == 0 and k % NCH:
                        act.wait_ge(acc_full, 2 * a_at["w", k - 1] + 2)
                    nc.scalar.activation(ho_t[:, kc, :], ps[:, kc, :], ACT.Copy).then_inc(tp_read, 1)

            def split(u):
                width, c, _ = split_unit(u)
                src = ps[:, unit_bank(u), 0:width]
                act.wait_ge(ring_full, u + 1)
                at_least(act, split_v, 3 * (u - 2) + 3)
                nc.scalar.activation(full[:, u % 2, 0:width], src, ACT.Identity, bias=col[:, c:c + 1])\
                    .then_inc(split_a, 1)
                if u >= 4:
                    act.wait_ge(parts_out[u % 4], parts_landed(u - 4))
                nc.scalar.activation(parts[:, u % 4, 0, 0:width], src, ACT.Identity, bias=col[:, c:c + 1])\
                    .then_inc(split_a, 1)

            def attention(a, s):
                def exp(g, u):
                    ui, h, k = a.units[u]
                    unit, width = len(a.units) * g + u, a.unit_width(u)
                    if u == 0 or a.units[u - 1][0] != ui:
                        at_least(act, s.pv, a.n_steps * g + ui - P_SLOTS + 1)
                    act.wait_ge(s.scores, unit + 1)
                    nc.scalar.activation(probs[0:a.kp, a.probs_slot(g, ui), h, k * BANK:k * BANK + width],
                                         ps[0:a.kp, unit % S_BANKS, 0:width], ACT.Exp, scale=SCALE)\
                        .then_inc(s.exps, 1)

                def copy_out(g):
                    act.wait_ge(s.pv, a.n_steps * (g + 1))
                    if g:
                        act.wait_ge(s.max_full, a.use_at["out", g - 1, 1] + 1)
                    nc.scalar.activation(out_t[:, :], out_region, ACT.Copy).then_inc(s.out_copied, 1)

                for op, *what in a.pe:
                    if op == "score":
                        exp(*what)
                    if op == "score" and a.step_end(*what) == 0 and what[0]:
                        copy_out(what[0] - 1)
                copy_out(NG - 1)

            act.wait_ge(col_in, 16)
            for k in range(NCH):
                copy_norm(k)
                if k:
                    for u in range(4):
                        split(4 * (k - 1) + u)
            for u in range(4):
                split(4 * (NCH - 1) + u)
            for u in range(2):
                split(U_KC + u)
            act.wait_ge(split_v, 3 * U_QC)
            act.wait_ge(acc_full, 2 * a_at["vc", 0] + 2)
            act.wait_ge(tp_full, 2 * NCH)
            attention(SELF, S1)
            act.wait_ge(S1.max_full, len(SELF.uses))
            copy_heads(NCH)
            for n in range(NCH + 1):
                if n + 1 < NCH:
                    copy_heads(NCH + n + 1)
                if n:
                    copy_norm(NCH + n - 1)
                    for u in range(2):
                        split(U_QC + 2 * (n - 1) + u)
            act.wait_ge(split_v, 3 * U_H)
            act.wait_ge(ring_full, U_H)
            attention(CROSS, S2)
            act.wait_ge(S2.max_full, len(CROSS.uses))

            def hidden(n):
                if n:
                    act.wait_ge(acc_full, 2 * a_at["f", n - 1] + 2)
                for f in range(FF // P):
                    u = U_H + n * (FF // P) + f
                    act.wait_ge(ring_full, u + 1)
                    nc.scalar.activation(hid_r[:, HI, f, :], ps[:, 2 + u % 4, :], ACT.Relu,
                                         bias=col[:, BF1 + f:BF1 + f + 1]).then_inc(hid_full, 1)
                    at_least(act, hid_low, u - U_H - 1)
                    nc.scalar.activation(full[:, u % 2, :], ps[:, 2 + u % 4, :], ACT.Relu,
                                         bias=col[:, BF1 + f:BF1 + f + 1]).then_inc(hid_done, 1)

            copy_heads(2 * NCH)
            copy_heads(2 * NCH + 1)
            for n in range(NCH):
                copy_norm(2 * NCH + n)
                if n + 2 < NCH:
                    copy_heads(2 * NCH + n + 2)
                hidden(n)

        @block.tensor
        def _(pe):
            def turn_norm(k):
                i, p = t_at["x", k], k % 2
                pe.wait_ge(ln_done, CT * (k + 1))
                for kc in range(KC):
                    at_least(pe, tp_read, 2 * (i - 1) + kc + 1)
                    for j in range(CT):
                        ins = nc.tensor.transpose(ps[:, kc, j * P:(j + 1) * P], xn[:, p, j, kc * P:(kc + 1) * P],
                                                  identf[:, :])
                    ins.then_inc(tp_full, 1)

            def turn_heads(k):
                i, n = t_at["o", k], k % NCH
                b, i0 = n // 2, (n % 2) * CT
                for kc in range(KC):
                    at_least(pe, tp_read, 2 * (i - 1) + kc + 1)
                    for j in range(CT):
                        ins = nc.tensor.transpose(ps[:, kc, j * P:(j + 1) * P],
                                                  heads_out[:, KC * b + kc, i0 + j, :], identf[:, :])
                    ins.then_inc(tp_full, 1)

            def ring_free(u):
                if u < U_KC:
                    n, c = divmod(u, 4)
                    if c in (1, 2) and n:
                        pe.wait_ge(acc_read, 2 * a_at["v", n - 1] + c)
                    elif c == 3 or c == 0 and n:
                        pe.wait_ge(split_a, 2 * (u - 3 if c else u - 1) + 2)
                elif u < U_QC:
                    if u == U_KC:
                        pe.wait_ge(split_a, 2 * U_KC)
                    else:
                        pe.wait_ge(acc_read, 2 * a_at["v", NCH - 1] + 1)
                elif u < U_H:
                    n, hh = divmod(u - U_QC, 2)
                    if hh:
                        pe.wait_ge(acc_read, 2 * a_at["w", NCH + min(n + 1, NCH - 1)] + 1)
                    elif n:
                        pe.wait_ge(split_a, 2 * (u - 2) + 2)
                elif u - 4 >= U_H:
                    pe.wait_ge(hid_done, u - 4 - U_H + 1)

            def project(u, k, weights, rhs, width):
                ring_free(u)
                for kc in range(KC):
                    ins = nc.tensor.matmul(ps[:, unit_bank(u), 0:width], weights(kc), rhs(kc),
                                           start=(kc == 0), stop=(kc == KC - 1))
                ins.then_inc(ring_full, 1)

            def rows_product(key, lhs_t, rhs, n_k):
                i = a_at[key]
                for half in range(2):
                    at_least(pe, acc_read, 2 * (i - 1) + half + 1)
                    if key[0] == "v":
                        pe.wait_ge(split_a, 2 * (4 * key[1] + 1 + half) + 2)
                    if half == 0 and key[0] == "w" and NCH + 2 <= key[1] < 2 * NCH:
                        pe.wait_ge(split_a, 2 * (U_QC + 2 * (key[1] - NCH - 2) + 1) + 2)
                    for j in (2 * half, 2 * half + 1):
                        for k in range(n_k):
                            ins = nc.tensor.matmul(acc[:, j, :], lhs_t(k, j), rhs(k), start=(k == 0),
                                                   stop=(k == n_k - 1))
                    ins.then_inc(acc_full, 1)

            def qkv(n):
                p = n % 2
                if n == 0:
                    pe.wait_ge(wqkv_in, 16)
                pe.wait_ge(tp_read, 2 * t_at["x", n] + 2)
                for s in range(4):
                    project(4 * n + s, n, lambda kc: wqkv[:, kc, s * P:(s + 1) * P],
                            lambda kc: xn_t[:, p, kc, :], CHUNK)
                    if n == NCH - 1:
                        attention(SELF, S1, SELF_EARLY[s], SELF_EARLY[s + 1])
                rows_product(("v", n), lambda k, j: xn_t[:, p, k, j * P:(j + 1) * P],
                             lambda k: wqkv[:, k, 2 * C:3 * C], KC)

            def context():
                pe.wait_ge(ctx_in, 32)
                for hh in range(2):
                    project(U_KC + hh, 0, lambda kc: wctx[:, kc, hh * P:(hh + 1) * P], lambda kc: ctxt[:, kc, :],
                            B * S_CTX)
                i = a_at["vc", 0]
                pe.wait_ge(acc_read, 2 * i)
                pe.wait_ge(split_a, 2 * U_QC)
                for b in range(B):
                    for kc in range(KC):
                        ins = nc.tensor.matmul(acc[0:S_CTX, 2 * b, :], ctxt[:, kc, b * S_CTX:(b + 1) * S_CTX],
                                               wctx[:, kc, C:2 * C], start=(kc == 0), stop=(kc == KC - 1))
                    ins.then_inc(acc_full, 1)

            def attention(a, s, lo, hi=None):
                def k_rows(n, g, h, lo, hi):
                    return (k_self[0:n, g % a.nb, h, lo:hi] if a.causal else k_ctx[0:n, g, h, lo:hi])

                def chunk(use, g, c):
                    t, h0, nh, s0, w = a.chunks[c]
                    if c == 0:
                        pe.wait_ge(s.q_in[g % a.nb], 16 * len(QP) * (1 + a.causal) * (g // a.nb + 1))
                        if g == 0 and not a.causal:
                            pe.wait_ge(s.k_in, 16 * len(KP))
                    diagonal = a.causal and s0 + w == (t + 1) * P
                    for h in range(h0, h0 + nh):
                        o = (h - h0) * w
                        ins = nc.tensor.matmul(m_bank(use)[:, o:o + w],
                                               q_stack[0:ROWS, g % a.nb, h, t * P:(t + 1) * P],
                                               k_rows(ROWS, g, h, s0, s0 + w), start=True, stop=not diagonal)
                        if diagonal:
                            ins = nc.tensor.matmul(m_bank(use)[:, o + w - P:o + w], identb[:, :], maskb[:, :],
                                                   start=False, stop=True)
                    return ins

                def shift_rows(use, g):
                    pe.wait_ge(s.shift_step, 5 * (g + 1))
                    dst = m_bank(use).bitcast(BF16)[0:PARTS * GH * TILES, 0:P]
                    return nc.tensor.transpose(dst, shift[:, :, :].rearrange("p a b -> p (a b)"), identb[:, :])

                def out_rows(use, g, half):
                    pe.wait_ge(s.out_copied, g + 1)
                    for j in range(4):
                        i = 4 * half + j
                        ins = nc.tensor.transpose(m_bank(use)[:, j * P:(j + 1) * P], out_t[:, i * P:(i + 1) * P],
                                                  identf[:, :])
                    return ins

                def score(g, u):
                    ui, h, k = a.units[u]
                    unit = len(a.units) * g + u
                    if u == 0:
                        pe.wait_ge(s.shift_in[g % a.nb], 16 * PARTS * (g // a.nb + 1))
                    at_least(pe, s.exps, unit - S_BANKS + 1)
                    for i, q0, w, off in a.steps[ui][0]:
                        lo, hi = max(off, k * BANK), min(off + w, (k + 1) * BANK)
                        if lo < hi:
                            keys = min(P, a.keys - i * P)
                            ins = nc.tensor.matmul(ps[0:keys, unit % S_BANKS, lo - k * BANK:hi - k * BANK],
                                                   k_rows(ROWS_S, g, h, i * P, i * P + keys),
                                                   q_stack[:, g % a.nb, h, q0 + lo - off:q0 + hi - off],
                                                   start=True, stop=True)
                    ins.then_inc(s.scores, 1)

                def product(g, ui):
                    if a.causal:
                        pe.wait_ge(s.masked, a.masks(g, ui))
                    else:
                        pe.wait_ge(s.exps, a.unit_index(g, ui + 1))
                    if ui == 0:
                        pe.wait_ge(s.v_set, g + 1 if a.causal else 1)
                        at_least(pe, s.out_copied, g)
                    slot = a.probs_slot(g, ui)
                    for i, q0, w, off in a.steps[ui][0]:
                        for bank in range(2):
                            lo, hi = max(q0, BANK * bank), BANK * (bank + 1)
                            if lo >= hi:
                                continue
                            last = i == a.kt - 1 or a.causal and bank == 0 and i == 3
                            for h in range(GH):
                                v = v_group[0:a.kp, g % 3, i, h, :] if a.causal else v_group[0:a.kp, 0, g, h, :]
                                o = off + lo - q0
                                ins = nc.tensor.matmul(out_region[32 * h:32 * h + 32, lo:hi], v,
                                                       probs[0:a.kp, slot, h, o:o + hi - lo],
                                                       start=(i == 0), stop=last, skip_group_check=True)
                    ins.then_inc(s.pv, 1)

                for op, *what in a.pe[lo:hi]:
                    if op == "score":
                        score(*what)
                    elif op == "product":
                        product(*what)
                    else:
                        use = what[0]
                        kind, *of = a.uses[use]
                        at_least(pe, s.max_read, use - M_BANKS + 1)
                        {"chunk": chunk, "shift": shift_rows, "out": out_rows}[kind](use, *of)\
                            .then_inc(s.max_full, 1)

            pe.wait_ge(consts, 7)
            for k in range(NCH):
                turn_norm(k)
                if k:
                    qkv(k - 1)
            attention(SELF, S1, 0, SELF_EARLY[0])
            qkv(NCH - 1)
            attention(SELF, S1, SELF_EARLY[4], SELF_EARLY[5])
            context()
            attention(SELF, S1, SELF_EARLY[5], SELF_EARLY[6])
            pe.wait_ge(split_a, 2 * U_QC)
            pe.wait_ge(acc_read, 2 * a_at["vc", 0] + 2)
            pe.wait_ge(consts, 9)
            attention(SELF, S1, SELF_EARLY[6])
            pe.wait_ge(S1.max_read, len(SELF.uses))
            pe.wait_ge(mid_in, 16)
            turn_heads(NCH)
            for n in range(NCH + 1):
                if n < NCH:
                    pe.wait_ge(tp_read, 2 * t_at["o", NCH + n] + 2)
                    rows_product(("w", NCH + n), lambda k, j: ho_t[:, k, j * P:(j + 1) * P],
                                 lambda k: wmid[:, k, W1:W1 + C], KC)
                if n + 1 < NCH:
                    turn_heads(NCH + n + 1)
                if n:
                    k = NCH + n - 1
                    if n == NCH:
                        attention(CROSS, S2, 0, CROSS_EARLY[0])
                    turn_norm(k)
                    if n == NCH:
                        attention(CROSS, S2, CROSS_EARLY[0], CROSS_EARLY[1])
                    pe.wait_ge(tp_read, 2 * t_at["x", k] + 2)
                    for hh in range(2):
                        project(U_QC + 2 * (n - 1) + hh, k,
                                lambda kc: wmid[:, kc, WQ_C + hh * P:WQ_C + (hh + 1) * P],
                                lambda kc: xn_t[:, k % 2, kc, :], CHUNK)
            pe.wait_ge(split_a, 2 * U_H)
            attention(CROSS, S2, CROSS_EARLY[1])
            pe.wait_ge(S2.max_read, len(CROSS.uses))
            pe.wait_ge(wf1_halves, 2)

            def feed_out(n):
                pe.wait_ge(hid_low, (FF // P) * (n + 1))
                if n == 0:
                    pe.wait_ge(wf2_halves, 2)
                terms = [(k, hw, hx) for k in range(FF // P) for hx, hw in PASSES]
                rows_product(("f", n), lambda t, j: hid_r[:, terms[t][2], terms[t][0], j * P:(j + 1) * P],
                             lambda t: wf2r[:, terms[t][1], terms[t][0], :], len(terms))

            def rows_w2(n):
                k = 2 * NCH + n
                pe.wait_ge(tp_read, 2 * t_at["o", k] + 2)
                rows_product(("w", k), lambda kk, j: ho_t[:, kk, j * P:(j + 1) * P],
                             lambda kk: wmid[:, kk, W2:W2 + C], KC)

            def hidden(n):
                k = 2 * NCH + n
                pe.wait_ge(xn_low, KC * (n + 1))
                for f in range(FF // P):
                    u = U_H + n * (FF // P) + f
                    ring_free(u)
                    terms = [(kc, hw, hx) for kc in range(KC) for hw, hx in PASSES]
                    for i, (kc, hw, hx) in enumerate(terms):
                        ins = nc.tensor.matmul(ps[:, 2 + u % 4, :], wf1r[:, hw, kc, f * P:(f + 1) * P],
                                               xn_r[:, hx, k % 2, kc, :], start=(i == 0),
                                               stop=(i == len(terms) - 1))
                    ins.then_inc(ring_full, 1)

            turn_heads(2 * NCH)
            rows_w2(0)
            turn_heads(2 * NCH + 1)
            rows_w2(1)
            turn_norm(2 * NCH)
            turn_heads(2 * NCH + 2)
            for n in range(NCH):
                hidden(n)
                if n + 1 < NCH:
                    turn_norm(2 * NCH + n + 1)
                feed_out(n)
                if n + 2 < NCH:
                    rows_w2(n + 2)
                if n + 3 < NCH:
                    turn_heads(2 * NCH + n + 3)

        @block.vector
        def _(dve):
            def ln_sums(k):
                n, p = k % NCH, k % 2
                at_least(dve, ln_var, k)
                at_least(dve, ln_done, CT * (k - 1))
                for j in range(CT):
                    nc.vector.bn_stats(stats[:, j, :], xs[:, n * CT + j, :]).then_inc(ln_stats, 1)
                dve.wait_ge(ln_stats, CT * (k + 1))
                for j in range(CT):
                    ins = nc.vector.bn_aggr(mean_var[:, p, j, :], stats[:, j, :])
                ins.then_inc(ln_var, 1)

            def ln_apply(k):
                n, p = k % NCH, k % 2
                dve.wait_ge(ln_rstd, k + 1)
                if 2 <= k < NCH or NCH + 2 <= k < 2 * NCH or 2 * NCH + 2 <= k:
                    dve.wait_ge(tp_full, 2 * t_at["x", k - 2] + 2)
                for j in range(CT):
                    nc.vector.tensor_scalar(xn[:, p, j, :], xs[:, n * CT + j, :], mean_var[:, p, j, 0:1],
                                            rstd[:, p, j:j + 1], ALU.subtract, ALU.mult).then_inc(ln_done, 1)

            def split(u):
                width, _, _ = split_unit(u)
                p, f = parts[:, u % 4, :, 0:width], full[:, u % 2, 0:width]
                r = rest[:, u % 2, 0:width]
                dve.wait_ge(split_a, 2 * u + 2)
                nc.vector.tensor_tensor(r, f, p[:, 0, :], ALU.subtract).then_inc(split_v, 1)
                dve.wait_ge(split_v, 3 * u + 1)
                nc.vector.tensor_copy(p[:, 1, :], r).then_inc(split_v, 1)
                dve.wait_ge(split_v, 3 * u + 2)
                nc.vector.tensor_tensor(p[:, 2, :], r, p[:, 1, :], ALU.subtract).then_inc(split_v, 1)

            def add_v(n):
                b, i0 = n // 2, (n % 2) * CT
                for half in range(2):
                    dve.wait_ge(acc_full, 2 * a_at["v", n] + half + 1)
                    for j in (2 * half, 2 * half + 1):
                        dst = v_self[:, 4 * b:4 * b + 4, i0 + j, :]
                        ins = nc.vector.tensor_tensor(dst, acc[:, j, :].rearrange("p (g c) -> p g c", g=4),
                                                      row[:, BV_S, :].rearrange("p (g c) -> p g c", g=4), ALU.add)
                    ins.then_inc(acc_read, 1)

            def add_rows(key, n, bias_k):
                i = a_at[key]
                dve.wait_ge(bias_added, bias_k + 1)
                for half in range(2):
                    dve.wait_ge(acc_full, 2 * i + half + 1)
                    t0 = n * CT + 2 * half
                    xt = xs[:, t0:t0 + 2, :]
                    nc.vector.tensor_tensor(xt, acc[:, 2 * half:2 * half + 2, :], xt, ALU.add)\
                        .then_inc(acc_read, 1)
                dve.wait_ge(acc_read, 2 * i + 2)

            def attention(a, s, lo, hi=None):
                def chunk(use, g, c):
                    t, h0, nh, s0, w = a.chunks[c]
                    p = g % 2
                    if c == 0:
                        at_least(dve, s.shift_step, 5 * (g - 2) + 1)
                        at_least(dve, s.maxima, g - 1)
                    dst = max_b[:, p, h0:h0 + nh, t - 4:t - 3] if s0 else max_a[:, p, h0:h0 + nh, t:t + 1]
                    nc.vector.tensor_reduce(dst, m_bank(use)[:, 0:nh * w].rearrange("p (h w) -> p h w", h=nh),
                                            AX.X, ALU.max).then_inc(s.max_read, 1)
                    if c + 1 == len(a.chunks):
                        dve.wait_ge(s.max_read, use + 1)
                        late = max_a[:, p, :, 4:8]
                        nc.vector.tensor_tensor(late, late, max_b[:, p, :, :] if a.causal else late, ALU.max)\
                            .then_inc(s.maxima, 1)

                def shift_rows(use, g):
                    if g:
                        dve.wait_ge(s.shift_in[(g - 1) % a.nb], 16 * PARTS * ((g - 1) // a.nb + 1))
                    src = m_bank(use).bitcast(BF16)[0:PARTS * GH * TILES, 0:P]
                    nc.vector.tensor_copy(shift_t[:, :], src).then_inc(s.max_read, 1)

                def out_rows(use, g, half):
                    bank = m_bank(use).rearrange("p (u c) -> p u c", c=32)
                    nc.vector.reciprocal(recip[:, half, :], bank[:, :, D]).then_inc(s.recips, 1)
                    dve.wait_ge(s.recips, 2 * g + half + 1)
                    dst = heads_out[:, g // 2, 4 * half:4 * half + 4, g % 2 * GW:g % 2 * GW + GW]
                    nc.vector.tensor_tensor(dst.rearrange("p i (h d) -> p i h d", d=D),
                                            bank[:, :, 0:D].rearrange("p (i h) d -> p i h d", h=GH),
                                            recip[:, half, :].rearrange("p (i h o) -> p i h o", h=GH, o=1)
                                            .to_broadcast([P, 4, GH, D]), ALU.mult).then_inc(s.max_read, 1)

                for use, (kind, *of) in list(enumerate(a.uses))[lo:hi]:
                    dve.wait_ge(s.max_full, use + 1)
                    {"chunk": chunk, "shift": shift_rows, "out": out_rows}[kind](use, *of)

            dve.wait_ge(x_in[0], 16)
            ln_sums(0)
            for n in range(NCH):
                if n + 1 < NCH:
                    dve.wait_ge(x_in[n + 1], 16)
                    ln_sums(n + 1)
                ln_apply(n)
                if n == 0:
                    dve.wait_ge(row_in, 16)
                if n:
                    for u in range(4):
                        split(4 * (n - 1) + u)
                    add_v(n - 1)
            attention(SELF, S1, 0, SELF_EARLY[0])
            for u in range(4):
                attention(SELF, S1, SELF_EARLY[u], SELF_EARLY[u + 1])
                split(4 * (NCH - 1) + u)
            add_v(NCH - 1)
            attention(SELF, S1, SELF_EARLY[4], SELF_EARLY[5])
            for u in range(2):
                split(U_KC + u)
            for b in range(B):
                dve.wait_ge(acc_full, 2 * a_at["vc", 0] + b + 1)
                nc.vector.tensor_tensor(v_ctx[:, 4 * b:4 * b + 4, :],
                                        acc[0:S_CTX, 2 * b, :].rearrange("p (g c) -> p g c", g=4),
                                        row[0:S_CTX, BV_C, :].rearrange("p (g c) -> p g c", g=4), ALU.add)\
                    .then_inc(acc_read, 1)
            attention(SELF, S1, SELF_EARLY[5])
            dve.wait_ge(S1.pv, SELF.n_steps * NG)
            for n in range(NCH + 2):
                if n < NCH:
                    add_rows(("w", NCH + n), n, n)
                    ln_sums(NCH + n)
                if n == NCH + 1:
                    attention(CROSS, S2, CROSS_EARLY[0], CROSS_EARLY[1])
                if n >= 2:
                    for u in range(2):
                        split(U_QC + 2 * (n - 2) + u)
                if n == NCH:
                    attention(CROSS, S2, 0, CROSS_EARLY[0])
                if n < NCH:
                    ln_apply(NCH + n)
            attention(CROSS, S2, CROSS_EARLY[1])
            dve.wait_ge(S2.pv, CROSS.n_steps * NG)

            def xn_low_half(n):
                k = 2 * NCH + n
                for kc in range(KC):
                    dve.wait_ge(tp_read, 2 * t_at["x", k] + kc + 1)
                    nc.vector.tensor_tensor(xn_r[:, LO, k % 2, kc, :], xn_t[:, k % 2, kc, :],
                                            xn_r[:, HI, k % 2, kc, :], ALU.subtract).then_inc(xn_low, 1)

            def hidden_low_halves(n, fs):
                for f in fs:
                    u = n * (FF // P) + f
                    dve.wait_ge(hid_done, u + 1)
                    nc.vector.tensor_tensor(hid_r[:, LO, f, :], full[:, (U_H + u) % 2, :], hid_r[:, HI, f, :],
                                            ALU.subtract).then_inc(hid_low, 1)

            for n in range(2):
                add_rows(("w", 2 * NCH + n), n, NCH + n)
                ln_sums(2 * NCH + n)
                ln_apply(2 * NCH + n)
            xn_low_half(0)
            for n in range(NCH):
                if n and n + 1 < NCH:
                    add_rows(("w", 2 * NCH + n + 1), n + 1, NCH + n + 1)
                    ln_sums(2 * NCH + n + 1)
                    hidden_low_halves(n, range(0, 4))
                    ln_apply(2 * NCH + n + 1)
                    hidden_low_halves(n, range(4, FF // P))
                else:
                    hidden_low_halves(n, range(FF // P))
                if n + 1 < NCH:
                    xn_low_half(n + 1)
                add_rows(("f", n), n, 2 * NCH + n)


def kernel(x, ctx_1024, **w):
    import numpy as np
    import concourse.bacc as bacc
    from concourse.bass_utils import run_bass_kernel_spmd as run

    w = {k.removeprefix("L0_xattn_"): np.asarray(v) for k, v in w.items()}

    def flat(name):
        return w[name].transpose(1, 0, 2).reshape(C, H * D)

    def channel_cols(v):
        return v.reshape(-1, P).T

    arrays = {
        "x": np.asarray(x),
        "w_qkv": np.concatenate([flat("Wq_s"), flat("Wk_s"), flat("Wv_s")], 1),
        "w_ctx": np.concatenate([flat("Wk_c"), flat("Wv_c")], 1),
        "w_mid": np.concatenate([w["W1"], flat("Wq_c"), w["W2"]], 1),
        "w_f1": w["Wf1"],
        "w_f2": w["Wf2"],
        "ctx_t": np.asarray(ctx_1024).reshape(B * S_CTX, C).T,
        "cols": np.concatenate([channel_cols(w[k]) for k in
                                ("bq_s", "bk_s", "bq_c", "bk_c", "g1", "be1", "g2", "be2", "g3", "be3", "bf1")], 1),
        "rows": np.stack([w[k].reshape(C) for k in ("bv_s", "b1", "bv_c", "b2", "bf2")]),
    }
    arrays = {k: np.ascontiguousarray(v) for k, v in arrays.items()}
    nc = bacc.Bacc("TRN2", target_bir_lowering=False, num_devices=1)
    args = [nc.dram_tensor(f"in_{k}", v.shape, mybir.dt.from_np(v.dtype), kind="ExternalInput").ap()
            for k, v in arrays.items()]
    out = nc.dram_tensor("out", (B, T, C), F32, kind="ExternalOutput").ap()
    build(nc, *args, out)
    r = run(nc, [{f"in_{k}": v for k, v in arrays.items()}], core_ids=[0])
    return r.results[0]["out"]
```

```python
from contextlib import ExitStack

import concourse.bass as bass
from concourse import mybir

ALU = mybir.AluOpType
ACT = mybir.ActivationFunctionType
AX = mybir.AxisListType
F32 = mybir.dt.float32
F32R = mybir.dt.float32r
BF16 = mybir.dt.bfloat16

P = 128
B, T, C, H, D = 2, 1024, 256, 16, 16
S_CTX = 77
FF = 4 * C
EPS = 1e-5
HI, LO = 0, 1
PASSES = [(HI, HI), (HI, LO), (LO, HI)]
KC = C // P
CHUNK = 512
CT = CHUNK // P
NCH = B * T // CHUNK
TILES = T // P
GH = 4
NG = B * H // GH
GW = GH * D
PARTS = 3
QP = [0, 0, 0, 1, 1, 2]
KP = [0, 1, 2, 0, 1, 0]
ROWS = D * len(QP)
ROWS_S = ROWS + PARTS
SCALE = float(D) ** 0.5
NEG = -1e30
BANK = 512
M_BANKS = 3
S_BANKS = 3
P_SLOTS = 3

BQ_S, BK_S, BQ_C, BK_C, G1, BE1, G2, BE2, G3, BE3, BF1 = 0, 2, 4, 6, 8, 10, 12, 14, 16, 18, 20
NCOLS = 20 + FF // P
BV_S, B1, BV_C, B2, BF2 = range(5)
W1, WQ_C, W2 = 0, C, 2 * C


class Attention:

    def __init__(self, causal, keys, buffers, lead, gap, rows):
        self.causal, self.keys, self.nb = causal, keys, buffers
        self.kt = -(-keys // P)
        self.kp = min(P, keys)
        self.steps = []
        for tiles in ([[0], [1], [2], [3], [4, 5], [6, 7]] if causal else [[0]]):
            off, pieces = 0, []
            for i in tiles:
                w = T - i * P if causal else T
                pieces.append((i, T - w, w, off))
                off += w
            self.steps.append((pieces, off))
        self.n_steps = len(self.steps)
        self.units = [(ui, h, k) for ui, (_, width) in enumerate(self.steps)
                      for h in range(GH) for k in range(-(-width // BANK))]
        self.chunks = []
        for t in range(TILES):
            keys_t = (t + 1) * P if causal else keys
            for s in range(0, keys_t, BANK):
                w = min(BANK, keys_t - s)
                nh = min(BANK // w, GH)
                self.chunks += [(t, h, nh, s, w) for h in range(0, GH, nh)]
        if causal:
            ends = [max(u for u, (ui, _, _) in enumerate(self.units) if ui == step) for step in (2, 3, 3, 3, 5)]
            self.moves = dict(zip(("loaded", "inverted", "stored", "spread", "divided"), ((1, u) for u in ends)))
        else:
            self.moves = {"loaded": (2, 4), "inverted": (3, 0), "stored": (3, 1), "spread": (3, 3), "divided": (3, 6)}
        self.order(lead, gap, rows)

    def order(self, lead, gap, rows):
        def spread(costs):
            total, at, out = sum(costs), 0.0, []
            for c in costs:
                out.append(at / total)
                at += c
            return out
        unit_at = spread([self.unit_width(u) + BANK for u in range(len(self.units))])
        chunk_at = spread([nh * w + 64 for _, _, nh, _, w in self.chunks])
        stream = [(g + chunk_at[c], ("chunk", g, c)) for g in range(NG) for c in range(len(self.chunks))]
        stream += [(g + 1 + gap, ("shift", g)) for g in range(NG)]
        for n, (first, second, normed) in enumerate(rows):
            stream += [(first + lead, ("rows", n, 0)), (second + lead, ("rows", n, 1)), (normed + lead, ("norm", n))]
        stream.sort(key=lambda e: e[0])
        self.pe, self.uses = [], []

        def use(what):
            if what[0] == "norm":
                self.pe.append(what)
                return
            self.pe.append(("m", len(self.uses)))
            self.uses.append(what)

        for g in range(NG):
            for u, (ui, h, k) in enumerate(self.units):
                while stream and stream[0][0] <= g + unit_at[u] + lead:
                    use(stream.pop(0)[1])
                self.pe.append(("score", g, u))
                if u + 1 == len(self.units) or self.units[u + 1][0] != ui:
                    if ui:
                        self.pe.append(("product", g, ui - 1))
                    elif g:
                        self.pe.append(("product", g - 1, self.n_steps - 1))
        for _, what in stream:
            use(what)
        self.pe.append(("product", NG - 1, self.n_steps - 1))
        self.use_at = {what: i for i, what in enumerate(self.uses)}

    def unit_width(self, u):
        ui, _, k = self.units[u]
        return min(BANK, self.steps[ui][1] - k * BANK)

    def unit_index(self, g, ui):
        return g * len(self.units) + sum(u[0] < ui for u in self.units)

    def behind(self, what, g, u):
        lag, unit = self.moves[what]
        return g - lag if g >= lag and u == unit else None

    def left(self, what):
        return range(NG - self.moves[what][0], NG)

    def step_end(self, g, u):
        ui = self.units[u][0]
        return ui if u + 1 == len(self.units) or self.units[u + 1][0] != ui else None

    def masks(self, g, ui):
        return self.kt * g + sum(len(pieces) for pieces, _ in self.steps[:ui + 1])

    def probs_slot(self, g, ui):
        return (self.n_steps * g + ui + (not self.causal)) % P_SLOTS


SELF = Attention(True, T, buffers=3, lead=1.35, gap=0.12, rows=[(6.8, 6.9, 7.15), (7.3, 7.4, 7.6)])
CROSS = Attention(False, S_CTX, buffers=5, lead=2.3, gap=0.5, rows=[(7.05, 7.15, 7.55), (7.6, 7.7, 7.99)])
SELF_EARLY = [14, 18, 22, 26, 30, 36, 44]
CROSS_EARLY = [12, 16]


def at_least(eng, sem, value):
    if not isinstance(value, int) or value > 0:
        eng.wait_ge(sem, value)


def build(nc, x, w_qkv, w_ctx, w_mid, w_f1, w_f2, ctx_t, cols, rows, out):
    x_d = x.rearrange("b t c -> (b t) c").rearrange("(n p) c -> p n c", p=P)
    out_d = out.rearrange("b t c -> (b t) c").rearrange("(n p) c -> p n c", p=P)
    q_dram = nc.dram_tensor("q_parts", (PARTS, NG, GW, T), BF16).ap()
    k_dram = nc.dram_tensor("k_parts", (PARTS, NG, GW, T), BF16).ap()
    qc_dram = nc.dram_tensor("qc_parts", (PARTS, NG, GW, T), BF16).ap()
    heads_dram = nc.dram_tensor("heads", (2, NG, GH, 2 * D, T), F32).ap()
    recip_dram = nc.dram_tensor("recip_rows", (2, NG // 2, 2 * GH, T), F32).ap()
    kc_dram = nc.dram_tensor("kc_parts", (PARTS, NG, GW, S_CTX), BF16).ap()

    with ExitStack() as ctx:
        def sb(name, shape, dt=F32):
            return ctx.enter_context(nc.sbuf_tensor(name, shape, dt))

        def sem(name):
            return ctx.enter_context(nc.semaphore(name))

        xs = sb("xs", [P, NCH * CT, C])
        wmid = sb("wmid", [P, KC, 3 * C])
        col = sb("col", [P, NCOLS])
        row = sb("row", [P, 5, C])
        identf = sb("identf", [P, P])
        identb = sb("identb", [P, P], BF16)
        maskb = sb("maskb", [P, P], BF16)
        neghalf = sb("neghalf", [P, CT])
        arena_h = sb("arena_h", [P, NG // 2 * T])
        heads_out = arena_h[:, :].rearrange("p (g t) -> p g t", g=NG // 2)
        recips = sb("recips", [P, T])
        sums = sb("sums", [P, 2 * GH * T // P])
        n_qkv, n_ctx = KC * 3 * C, KC * 2 * C
        wqkv = arena_h[:, 0:n_qkv].rearrange("p (k n) -> p k n", k=KC)
        wctx = arena_h[:, n_qkv:n_qkv + n_ctx].rearrange("p (k n) -> p k n", k=KC)
        ctxt = arena_h[:, n_qkv + n_ctx:n_qkv + n_ctx + KC * B * S_CTX].rearrange("p (k n) -> p k n", k=KC)
        with ExitStack() as self_only:
            arena_v = self_only.enter_context(nc.sbuf_tensor("arena_v", [P, NG * TILES * GW], F32))
        wf1_low = sb("wf1_low", [P, KC, FF], F32R)
        sb("wf2_place", [P, FF // P, C])
        v_self = arena_v[:, :].rearrange("p (g i c) -> p g i c", g=NG, i=TILES)
        wf1 = arena_v[:, 0:KC * FF].rearrange("p (k n) -> p k n", k=KC)
        wf2 = arena_v[:, KC * FF:2 * KC * FF].rearrange("p (k n) -> p k n", k=FF // P)
        v_ctx = sb("v_ctx", [S_CTX, NG, GW])
        wf1_high = sb("wf1_high", [P, KC, FF], F32R)
        wf1r = (wf1_high[:, :, :], wf1_low[:, :, :])
        v_group = sb("v_group", [P, 3, TILES, GH, 32])
        out_t = sb("out_t", [P, T])
        max_a = sb("max_a", [P, 2, GH, TILES])
        max_b = sb("max_b", [P, 2, GH, 4])
        neg_m = sb("neg_m", [P, GH * TILES])
        neg_r = sb("neg_r", [P, GH * TILES])
        shift = sb("shift", [P, PARTS, GH * TILES], BF16)
        shift_t = sb("shift_t", [PARTS * GH * TILES, P], BF16)
        parts = sb("parts", [P, 4, PARTS, CHUNK], BF16)
        stats = sb("stats", [P, CT, 6])
        mean_var = sb("mean_var", [P, 2, CT, 2])
        veps = sb("veps", [P, 2, CT])
        rstd = sb("rstd", [P, 2, CT])
        xn = sb("xn", [P, 2, CT, C])
        with ExitStack() as attention_only:
            stacks = attention_only.enter_context(nc.sbuf_tensor("stacks", [ROWS_S, 6, GH, T], BF16))
            arena_p = attention_only.enter_context(nc.sbuf_tensor("arena_p", [P, P_SLOTS * GH * T], F32))
        q_stack = stacks[:, 0:5, :, :]
        k_self = stacks[:, 3:6, :, :]
        k_ctx = stacks[:, 5, :, :].rearrange("p h t -> p (h t)")[:, 0:NG * GH * S_CTX]\
            .rearrange("p (g h t) -> p g h t", g=NG, h=GH)
        probs = arena_p[:, :].rearrange("p (s h t) -> p s h t", s=P_SLOTS, h=GH)
        wf2r = sb("wf2r", [P, 2, FF // P, C], F32R)
        hid_r = sb("hid_r", [P, 2, FF // P, CHUNK], F32R)
        xn_r = sb("xn_r", [P, 2, 2, KC, CHUNK], F32R)
        sb("scratch_place", [P, 4 * 1024])
        wqkv_r = sb("wqkv_r", [P, 2, KC, 3 * C], F32R)
        at = [4 * 1024]

        def scratch(*shape):
            n = 1
            for s in shape:
                n *= s
            a = arena_p[:, at[0]:at[0] + n]
            at[0] += n
            names = "abcd"[:len(shape)]
            if len(shape) == 1:
                return a
            return a.rearrange("p (" + " ".join(names) + ") -> p " + " ".join(names),
                               **{k: s for k, s in zip(names, shape)})
        xn_t = scratch(2, KC, CHUNK)
        full = scratch(2, CHUNK)
        rest = scratch(2, CHUNK)

        ps = ctx.enter_context(nc.psum_tensor("ps", [P, 8, 512], F32))
        acc = ps[:, 6:8, :].rearrange("p b (j c) -> p (b j) c", c=C)
        out_region = ps[:, 6:8, :].rearrange("p b n -> p (b n)")

        def m_bank(use):
            return ps[:, S_BANKS + use % M_BANKS, :]

        x_in = [sem(f"x_in{n}") for n in range(NCH)]
        wqkv_in, col_in, row_in, ctx_in, mid_in, ff_in = (sem(n) for n in
            ("wqkv_in", "col_in", "row_in", "ctx_in", "mid_in", "ff_in"))
        consts = sem("consts")
        ln_stats, ln_var, ln_veps, ln_rstd, ln_done = (sem(n) for n in
            ("ln_stats", "ln_var", "ln_veps", "ln_rstd", "ln_done"))
        bias_added = sem("bias_added")
        tp_full, tp_read = sem("tp_full"), sem("tp_read")
        ring_full = sem("ring_full")
        acc_full, acc_read = sem("acc_full"), sem("acc_read")
        split_a, split_v, split_p = sem("split_a"), sem("split_v"), sem("split_p")
        parts_out = [sem(f"parts_out{s}") for s in range(4)]
        wf1_halves, wf2_halves = sem("wf1_halves"), sem("wf2_halves")
        wqkv_halves, xn_low_a = sem("wqkv_halves"), sem("xn_low_a")
        xn_full, xn_low = sem("xn_full"), sem("xn_low")
        hid_full, hid_done, hid_low = sem("hid_full"), sem("hid_done"), sem("hid_low")
        out_done = sem("out_done")

        class Sems:
            def __init__(self, pre, a):
                s = lambda name: sem(f"{pre}_{name}")
                self.q_in = [s(f"q_in{p}") for p in range(a.nb)]
                self.k_in = s("k_in")
                self.shift_in = [s(f"shift_in{p}") for p in range(a.nb)]
                self.v_set = s("v_set")
                self.max_full, self.max_read = s("max_full"), s("max_read")
                self.maxima = s("maxima")
                self.shift_step = s("shift_step")
                self.scores, self.exps = s("scores"), s("exps")
                self.masked = s("masked")
                self.pv = s("pv")
                self.out_copied = s("out_copied")
                self.heads_stored = s("heads_stored")
                self.heads_in = s("heads_in")
                self.recips_done = s("recips_done")
                self.recips_stored, self.recips_in = s("recips_stored"), s("recips_in")
                self.heads_done = s("heads_done")
        S1, S2 = Sems("self", SELF), Sems("cross", CROSS)

        a_order = [("v", n) for n in range(NCH)] + [("vc", 0)] + [("w", NCH + n) for n in range(2, NCH)]
        for n in range(NCH):
            a_order.append(("f", n))
            if n + 2 < NCH:
                a_order.append(("w", 2 * NCH + n + 2))
        a_at = {key: i for i, key in enumerate(a_order)}
        U_KC, U_QC, U_H = 4 * NCH, 4 * NCH + 2, 4 * NCH + 2 + 2 * NCH

        def split_unit(u):
            if u < U_KC:
                n, s = divmod(u, 4)
                dst, c0 = (q_dram, BQ_S) if s < 2 else (k_dram, BK_S)
                hh = s % 2
            elif u < U_QC:
                hh = u - U_KC
                d = [kc_dram[:, 4 * b + 2 * hh:4 * b + 2 * hh + 2, :, :] for b in range(B)]
                return B * S_CTX, BK_C + hh, [(a.rearrange("p g r t -> (g r) p t"), b * S_CTX, S_CTX)
                                              for b, a in enumerate(d)]
            else:
                n, hh = divmod(u - U_QC, 2)
                dst, c0 = qc_dram, BQ_C
            b, t0 = n // 2, (n % 2) * CHUNK
            a = dst[:, 4 * b + 2 * hh:4 * b + 2 * hh + 2, :, t0:t0 + CHUNK]
            return CHUNK, c0 + hh, [(a.rearrange("p g r t -> (g r) p t"), 0, CHUNK)]

        def parts_landed(u):
            return 16 * sum(2 if U_KC <= v < U_QC else 1 for v in range(u % 4, u + 1, 4))

        def unit_bank(u):
            if u < U_KC:
                return (2, 6, 7, 2)[u % 4]
            return (2, 6)[u % 2] if u < U_H else 2 + u % 4

        block = ctx.enter_context(nc.Block())

        @block.sync
        def _(sp):
            sp.dma_start(xs[:, 0:CT, :], x_d[:, 0:CT, :]).then_inc(x_in[0], 16)
            sp.dma_start(col[:, :], cols).then_inc(col_in, 16)
            sp.dma_start(wqkv[:, :, :], w_qkv.rearrange("(k p) n -> p k n", p=P)).then_inc(wqkv_in, 16)
            for n in range(1, NCH):
                sp.dma_start(xs[:, n * CT:(n + 1) * CT, :], x_d[:, n * CT:(n + 1) * CT, :]).then_inc(x_in[n], 16)
                if n == 1:
                    sp.dma_start(row[:, :, :], rows.rearrange("(o r) c -> o r c", o=1).to_broadcast([P, 5, C]))\
                        .then_inc(row_in, 16)
            sp.dma_start(wctx[:, :, :], w_ctx.rearrange("(k p) n -> p k n", p=P)).then_inc(ctx_in, 16)
            sp.dma_start(ctxt[:, :, :], ctx_t.rearrange("(k p) n -> p k n", p=P)).then_inc(ctx_in, 16)
            sp.dma_start(wmid[:, :, :], w_mid.rearrange("(k p) n -> p k n", p=P)).then_inc(mid_in, 16)

            def store_parts(u):
                width, _, dsts = split_unit(u)
                sp.wait_ge(split_p, u + 1)
                for dst, c0, w in dsts:
                    sp.dma_start(dst, parts[:, u % 4, :, c0:c0 + w]).then_inc(parts_out[u % 4], 16)

            def load_blocks(src, dst, which, gs, arrived):
                for blk in range(len(QP)):
                    sp.dma_start(dst[blk * D:(blk + 1) * D],
                                 src[which[blk], gs, :, :].rearrange("g (h d) t -> d (g h) t", d=D))\
                        .then_inc(arrived, 16)

            def load_stacks(a, s, g):
                par = g % a.nb
                at_least(sp, s.scores, len(a.units) * (g - a.nb + 1))
                load_blocks(q_dram if a.causal else qc_dram, q_stack[:, par, :, :], QP, slice(g, g + 1), s.q_in[par])
                if a.causal:
                    load_blocks(k_dram, k_self[:, par, :, :], KP, slice(g, g + 1), s.q_in[par])

            def attention(a, s, lo, hi=None):
                def load_shift(g):
                    sp.wait_ge(s.max_read, a.use_at["shift", g] + 1)
                    for k in range(PARTS):
                        n = GH * TILES
                        dst = q_stack[ROWS + k:ROWS + k + 1, g % a.nb, :, :]
                        sp.dma_start(dst.rearrange("o h (i t) -> o (h i) t", t=P), shift_t[k * n:(k + 1) * n, :])\
                            .then_inc(s.shift_in[g % a.nb], 16)

                def load_heads(g):
                    if g % 2 == 0:
                        return
                    sp.wait_ge(s.heads_stored, 16 * (g + 1))
                    at_least(sp, s.heads_done, g // 2)
                    src = heads_dram[0 if a.causal else 1, g - 1:g + 1].rearrange("g h r t -> (g h) r t")
                    sp.dma_start(sums[:, :], src[:, D, :].rearrange("h (s c) -> h s c", c=sums.shape[1]))\
                        .then_inc(s.heads_in, 16)
                    sp.dma_start(heads_out[:, g // 2, :], src[:, 0:D, :]).then_inc(s.heads_in, 16)

                def store_recips(g):
                    if g % 2 == 0:
                        return
                    sp.wait_ge(s.recips_done, g // 2 + 1)
                    dst = recip_dram[0 if a.causal else 1, g // 2]
                    sp.dma_start(dst.rearrange("h (s c) -> (h s) c", c=sums.shape[1]), sums[:, :])\
                        .then_inc(s.recips_stored, 16)

                def spread_recips(g):
                    if g % 2 == 0:
                        return
                    dst = recip_dram[0 if a.causal else 1, g // 2]
                    sp.wait_ge(s.recips_stored, 16 * (g // 2 + 1))
                    at_least(sp, s.heads_done, g // 2)
                    sp.dma_start(recips[:, :], dst.rearrange("h (o t) -> h o t", o=1).to_broadcast([2 * GH, D, T]))\
                        .then_inc(s.recips_in, 16)

                for op, *what in a.pe[lo:hi]:
                    if op == "m" and a.uses[what[0]][0] == "shift":
                        load_shift(a.uses[what[0]][1])
                    if op == "score" and a.behind("loaded", *what) is not None:
                        load_heads(a.behind("loaded", *what))
                    if op == "score" and a.behind("stored", *what) is not None:
                        store_recips(a.behind("stored", *what))
                    if op == "score" and a.behind("spread", *what) is not None:
                        spread_recips(a.behind("spread", *what))
                    if a.causal and op == "score" and what[0] == NG - 1 and a.step_end(*what) == 1:
                        sp.wait_ge(S1.v_set, NG)
                        sp.dma_start(wf1, w_f1.rearrange("(k p) n -> p k n", p=P)).then_inc(ff_in, 16)
                        sp.dma_start(wf2, w_f2.rearrange("(k p) n -> p k n", p=P)).then_inc(ff_in, 16)
                    if op == "score" and what[1] + 1 == len(a.units):
                        if what[0] + a.nb < NG:
                            load_stacks(a, s, what[0] + a.nb)
                        if a.causal and what[0] == NG - 3:
                            sp.wait_ge(S1.scores, len(a.units) * (NG - 2))
                            load_blocks(kc_dram, k_ctx.rearrange("p g h t -> p (g h) t"), KP, slice(0, NG), S2.k_in)
                if hi is None:
                    for g in range(NG):
                        if g in a.left("loaded"):
                            load_heads(g)
                        if g in a.left("stored"):
                            store_recips(g)
                        if g in a.left("spread"):
                            spread_recips(g)

            def wait_parts(units):
                for slot in range(4):
                    sp.wait_ge(parts_out[slot], parts_landed(max(u for u in range(units) if u % 4 == slot)))

            for u in range(U_QC):
                if u == 2 * NCH:
                    wait_parts(2 * NCH)
                    load_stacks(SELF, S1, 0)
                if u == 3 * NCH:
                    load_stacks(SELF, S1, 1)
                store_parts(u)
            load_stacks(SELF, S1, 2)
            wait_parts(U_QC)
            attention(SELF, S1, 0)
            for n in range(NCH):
                if n == NCH - 1:
                    attention(CROSS, S2, 0, CROSS_EARLY[-1])
                store_parts(U_QC + 2 * n)
                store_parts(U_QC + 2 * n + 1)
                if n == 1:
                    wait_parts(U_QC + NCH)
                if n >= 1 and n < NCH - 1:
                    load_stacks(CROSS, S2, 2 * n - 2)
                    load_stacks(CROSS, S2, 2 * n - 1)
            wait_parts(U_H)
            load_stacks(CROSS, S2, 4)
            attention(CROSS, S2, CROSS_EARLY[-1])
            for n in range(NCH):
                for half in range(2):
                    sp.wait_ge(acc_read, 2 * a_at["f", n] + half + 1)
                    t0 = n * CT + 2 * half
                    sp.dma_start(out_d[:, t0:t0 + 2, :], xs[:, t0:t0 + 2, :]).then_inc(out_done, 16)
            sp.wait_ge(out_done, 16 * 2 * NCH)

        @block.gpsimd
        def _(pool):
            c = [0]

            def made(ins, n=1):
                ins.then_inc(consts, 1)
                c[0] += 1
            made(pool.memset(identf[:, :], 0.0))
            made(pool.memset(identb[:, :], 0.0))
            made(pool.memset(maskb[:, :], 0.0))
            made(pool.memset(neghalf[:, :], -0.5))
            pool.wait_ge(consts, 4)
            for m in (identf, identb):
                made(pool.affine_select(out=m[:, :], in_=m[:, :], compare_op=ALU.not_equal, fill=1.0, base=0,
                                        pattern=[[-1, P]], channel_multiplier=1))
            made(pool.affine_select(out=maskb[:, :], in_=maskb[:, :], compare_op=ALU.is_ge, fill=NEG, base=0,
                                    pattern=[[-1, P]], channel_multiplier=1))

            def ln_root(k):
                pool.wait_ge(ln_var, k + 1)
                pool.tensor_scalar(veps[:, k % 2, :], mean_var[:, k % 2, :, 1], EPS, None, ALU.add)\
                    .then_inc(ln_veps, 1)
                pool.wait_ge(ln_veps, k + 1)
                pool.tensor_tensor(rstd[:, k % 2, :], veps[:, k % 2, :], neghalf[:, :], ALU.pow)\
                    .then_inc(ln_rstd, 1)

            def add_bias(k):
                n = k % NCH
                r = (B1, B2, BF2)[k // NCH]
                pool.wait_ge(ln_done, CT * (k + 1))
                if k == 0:
                    pool.wait_ge(row_in, 16)
                for j in range(CT):
                    xt = xs[:, n * CT + j, :]
                    ins = pool.tensor_tensor(xt, xt, row[:, r, :], ALU.add)
                ins.then_inc(bias_added, 1)

            def third_parts(*units):
                for u in units:
                    width, _, _ = split_unit(u)
                    p = parts[:, u % 4, :, 0:width]
                    pool.wait_ge(split_v, 2 * u + 2)
                    pool.tensor_tensor(p[:, 2, :], rest[:, u % 2, 0:width], p[:, 1, :], ALU.subtract)\
                        .then_inc(split_p, 1)

            def weight_halves(high, low, w, done):
                pool.tensor_copy(high, w).then_inc(done, 1)
                pool.wait_ge(done, 1)
                pool.tensor_tensor(low, w, high, ALU.subtract).then_inc(done, 1)

            def attention(a, s, lo=0, hi=None):
                def set_v(g):
                    pool.wait_ge(acc_read, 2 * a_at["v", 1 + 2 * (g // (NG // B))] + 2 if a.causal
                                 else 2 * a_at["vc", 0] + 2)
                    if a.causal:
                        at_least(pool, s.pv, a.n_steps * (g - 2))
                        src = v_self[:, g, :, :].rearrange("p i (h d) -> p i h d", d=D)
                        dst = v_group[:, g % 3, :, :, 0:D]
                    else:
                        src = v_ctx[:, :, :].rearrange("p g (h d) -> p g h d", d=D)
                        dst = v_group[0:S_CTX, 0, :, :, 0:D]
                    pool.tensor_copy(dst, src).then_inc(s.v_set, 1)

                def split_shift(g):
                    pool.wait_ge(s.maxima, g + 1)
                    m = max_a[:, g % 2, :, :].rearrange("p h i -> p (h i)")
                    base = 5 * g
                    pool.tensor_scalar(neg_m[:, :], m, -1.0, None, ALU.mult).then_inc(s.shift_step, 1)
                    pool.wait_ge(s.shift_step, base + 1)
                    pool.tensor_copy(shift[:, 0, :], neg_m[:, :]).then_inc(s.shift_step, 1)
                    pool.wait_ge(s.shift_step, base + 2)
                    pool.tensor_tensor(neg_r[:, :], neg_m[:, :], shift[:, 0, :], ALU.subtract)\
                        .then_inc(s.shift_step, 1)
                    pool.wait_ge(s.shift_step, base + 3)
                    pool.tensor_copy(shift[:, 1, :], neg_r[:, :]).then_inc(s.shift_step, 1)
                    pool.wait_ge(s.shift_step, base + 4)
                    pool.tensor_tensor(shift[:, 2, :], neg_r[:, :], shift[:, 1, :], ALU.subtract)\
                        .then_inc(s.shift_step, 1)

                def mask(g, ui):
                    pool.wait_ge(s.exps, a.unit_index(g, ui + 1))
                    for i, q0, w, off in a.steps[ui][0]:
                        blk = probs[:, a.probs_slot(g, ui), :, off:off + P]
                        pool.affine_select(out=blk, in_=blk, compare_op=ALU.is_ge, fill=0.0, base=0,
                                           pattern=[[0, GH], [1, P]], channel_multiplier=-1).then_inc(s.masked, 1)

                if lo == 0:
                    set_v(0)
                for op, *what in a.pe[lo:hi]:
                    if op == "m" and a.uses[what[0]] == ("chunk", a.uses[what[0]][1], len(a.chunks) - 1):
                        g = a.uses[what[0]][1]
                        split_shift(g)
                        if not a.causal and g in (NG - 5, NG - 4):
                            add_bias(NCH + 2 + g - (NG - 5))
                        if not a.causal and g == NG - 1:
                            pool.wait_ge(ff_in, 32)
                            weight_halves(*wf1r, wf1, wf1_halves)
                    if op == "norm":
                        ln_root((NCH if a.causal else 2 * NCH) + what[0])
                    if op == "score" and a.causal and a.step_end(*what) is not None:
                        mask(what[0], a.step_end(*what))
                        if a.step_end(*what) == 0 and what[0] + 1 < NG:
                            set_v(what[0] + 1)

            made(pool.memset(v_group[:, :, :, :, D:32], 1.0))
            def low_half(k):
                for kc in range(KC):
                    pool.wait_ge(tp_read, 2 * k + kc + 1)
                    pool.tensor_tensor(xn_r[:, LO, k % 2, kc, :], xn_t[:, k % 2, kc, :], xn_r[:, HI, k % 2, kc, :],
                                       ALU.subtract).then_inc(xn_low_a, 1)

            ln_root(0)
            ln_root(1)
            low_half(0)
            ln_root(2)
            low_half(1)
            add_bias(0)
            third_parts(*range(0, 4))
            low_half(2)
            ln_root(3)
            add_bias(1)
            third_parts(*range(4, 8))
            low_half(3)
            add_bias(2)
            third_parts(*range(8, 12))
            add_bias(3)
            pool.wait_ge(bias_added, NCH)
            made(pool.memset(k_self[ROWS:ROWS_S, :, :, :], 1.0))
            pool.wait_ge(consts, 9)
            third_parts(*range(12, U_QC))
            attention(SELF, S1)
            add_bias(NCH)
            add_bias(NCH + 1)
            third_parts(*range(U_QC, U_QC + 4))
            ln_root(NCH + 2)
            ln_root(NCH + 3)
            third_parts(U_QC + 4, U_QC + 5)
            attention(CROSS, S2, 0, CROSS_EARLY[1])
            third_parts(U_QC + 6, U_QC + 7)
            attention(CROSS, S2, CROSS_EARLY[1])
            pool.wait_ge(S2.pv, CROSS.n_steps * NG)
            weight_halves(wf2r[:, HI], wf2r[:, LO], wf2, wf2_halves)
            add_bias(2 * NCH)
            add_bias(2 * NCH + 1)
            for k in range(2 * NCH + 2, 3 * NCH):
                ln_root(k)
                add_bias(k)

        @block.scalar
        def _(act):
            def copy_norm(k):
                i, p = k, k % 2
                gcol, bcol = ((G1, BE1), (G2, BE2), (G3, BE3))[k // NCH]
                for kc in range(KC):
                    act.wait_ge(tp_full, 2 * i + kc + 1)
                    if kc == 0 and 2 <= k < NCH:
                        act.wait_ge(acc_full, 2 * a_at["v", k - 2] + 2)
                    if kc == 0 and NCH + 2 <= k < 2 * NCH:
                        act.wait_ge(ring_full, U_QC + 2 * (k - NCH - 2) + 2)
                    if kc == 0 and 2 * NCH + 2 <= k:
                        act.wait_ge(ring_full, U_H + 8 * (k - 2 * NCH - 2) + 8)
                        act.wait_ge(xn_low, KC * (k - 2 * NCH - 1))
                    if kc == 0 and 2 <= k < NCH:
                        act.wait_ge(xn_low_a, KC * (k - 1))
                    if k >= 2 * NCH or k < NCH:
                        nc.scalar.activation(xn_r[:, HI, p, kc, :], ps[:, kc, :], ACT.Identity,
                                             scale=col[:, gcol + kc:gcol + kc + 1],
                                             bias=col[:, bcol + kc:bcol + kc + 1]).then_inc(xn_full, 1)
                    nc.scalar.activation(xn_t[:, p, kc, :], ps[:, kc, :], ACT.Identity,
                                         scale=col[:, gcol + kc:gcol + kc + 1],
                                         bias=col[:, bcol + kc:bcol + kc + 1]).then_inc(tp_read, 1)

            def split(u):
                width, c, _ = split_unit(u)
                src = ps[:, unit_bank(u), 0:width]
                act.wait_ge(ring_full, u + 1)
                at_least(act, split_v, 2 * (u - 2) + 1)
                nc.scalar.activation(full[:, u % 2, 0:width], src, ACT.Identity, bias=col[:, c:c + 1])\
                    .then_inc(split_a, 1)
                if u >= 4:
                    act.wait_ge(parts_out[u % 4], parts_landed(u - 4))
                nc.scalar.activation(parts[:, u % 4, 0, 0:width], src, ACT.Identity, bias=col[:, c:c + 1])\
                    .then_inc(split_a, 1)

            def attention(a, s):
                def exp(g, u):
                    ui, h, k = a.units[u]
                    unit, width = len(a.units) * g + u, a.unit_width(u)
                    if u == 0 or a.units[u - 1][0] != ui:
                        at_least(act, s.pv, a.n_steps * g + ui - P_SLOTS + 1)
                    act.wait_ge(s.scores, unit + 1)
                    nc.scalar.activation(probs[0:a.kp, a.probs_slot(g, ui), h, k * BANK:k * BANK + width],
                                         ps[0:a.kp, unit % S_BANKS, 0:width], ACT.Exp, scale=SCALE)\
                        .then_inc(s.exps, 1)

                def copy_out(g):
                    act.wait_ge(s.pv, a.n_steps * (g + 1))
                    at_least(act, s.heads_stored, 16 * g)
                    nc.scalar.activation(out_t[:, :], out_region, ACT.Copy).then_inc(s.out_copied, 1)

                def store_out(g):
                    act.wait_ge(s.out_copied, g + 1)
                    act.dma_start(heads_dram[0 if a.causal else 1, g].rearrange("h r t -> (h r) t"), out_t[:, :])\
                        .then_inc(s.heads_stored, 16)

                copied = None
                for op, *what in a.pe:
                    if op == "score":
                        exp(*what)
                        if copied is not None:
                            store_out(copied)
                            copied = None
                    if op == "score" and a.step_end(*what) == 0 and what[0]:
                        copied = what[0] - 1
                        copy_out(copied)
                if copied is not None:
                    store_out(copied)
                if not a.causal:
                    copy_norm(2 * NCH)
                copy_out(NG - 1)
                store_out(NG - 1)

            act.wait_ge(wqkv_in, 16)
            nc.scalar.activation(wqkv_r[:, HI], wqkv, ACT.Copy).then_inc(wqkv_halves, 1)
            act.wait_ge(col_in, 16)
            for k in range(NCH):
                copy_norm(k)
                if k:
                    for u in range(4):
                        split(4 * (k - 1) + u)
            for u in range(4):
                split(4 * (NCH - 1) + u)
            for u in range(2):
                split(U_KC + u)
            act.wait_ge(split_p, U_QC)
            act.wait_ge(acc_full, 2 * a_at["vc", 0] + 2)
            act.wait_ge(tp_full, 2 * NCH)
            attention(SELF, S1)
            copy_norm(NCH)
            copy_norm(NCH + 1)
            for n in range(NCH):
                if n >= 2:
                    copy_norm(NCH + n)
                for u in range(2):
                    split(U_QC + 2 * n + u)
            act.wait_ge(split_p, U_H)
            act.wait_ge(ring_full, U_H)
            attention(CROSS, S2)

            def hidden(n):
                if n:
                    act.wait_ge(acc_full, 2 * a_at["f", n - 1] + 2)
                for f in range(FF // P):
                    u = U_H + n * (FF // P) + f
                    act.wait_ge(ring_full, u + 1)
                    nc.scalar.activation(hid_r[:, HI, f, :], ps[:, 2 + u % 4, :], ACT.Relu,
                                         bias=col[:, BF1 + f:BF1 + f + 1]).then_inc(hid_full, 1)
                    at_least(act, hid_low, u - U_H - 1)
                    nc.scalar.activation(full[:, u % 2, :], ps[:, 2 + u % 4, :], ACT.Relu,
                                         bias=col[:, BF1 + f:BF1 + f + 1]).then_inc(hid_done, 1)

            for n in range(NCH):
                if n:
                    copy_norm(2 * NCH + n)
                hidden(n)

        @block.tensor
        def _(pe):
            def turn_norm(k):
                i, p = k, k % 2
                pe.wait_ge(ln_done, CT * (k + 1))
                for kc in range(KC):
                    at_least(pe, tp_read, 2 * (i - 1) + kc + 1)
                    for j in range(CT):
                        ins = nc.tensor.transpose(ps[:, kc, j * P:(j + 1) * P], xn[:, p, j, kc * P:(kc + 1) * P],
                                                  identf[:, :])
                    ins.then_inc(tp_full, 1)

            def ring_free(u):
                if u < U_KC:
                    n, c = divmod(u, 4)
                    if c in (1, 2) and n:
                        pe.wait_ge(acc_read, 2 * a_at["v", n - 1] + c)
                    elif c == 3 or c == 0 and n:
                        pe.wait_ge(split_a, 2 * (u - 3 if c else u - 1) + 2)
                elif u < U_QC:
                    if u == U_KC:
                        pe.wait_ge(split_a, 2 * U_KC)
                    else:
                        pe.wait_ge(acc_read, 2 * a_at["v", NCH - 1] + 1)
                elif u < U_H:
                    n, hh = divmod(u - U_QC, 2)
                    if hh and n >= 2:
                        pe.wait_ge(acc_read, 2 * a_at["w", 2 * NCH - 1] + 1)
                    if n:
                        pe.wait_ge(split_a, 2 * (u - 2) + 2)
                elif u - 4 >= U_H:
                    pe.wait_ge(hid_done, u - 4 - U_H + 1)

            def project(u, k, weights, rhs, width, n_terms=KC):
                ring_free(u)
                for t in range(n_terms):
                    ins = nc.tensor.matmul(ps[:, unit_bank(u), 0:width], weights(t), rhs(t),
                                           start=(t == 0), stop=(t == n_terms - 1))
                ins.then_inc(ring_full, 1)

            def rows_product(key, lhs_t, rhs, n_k):
                i = a_at[key]
                for half in range(2):
                    at_least(pe, acc_read, 2 * (i - 1) + half + 1)
                    if key[0] == "v":
                        pe.wait_ge(split_a, 2 * (4 * key[1] + 1 + half) + 2)
                    if half == 0 and key == ("w", NCH + 2):
                        pe.wait_ge(split_a, 2 * (U_QC + 3) + 2)
                    for j in (2 * half, 2 * half + 1):
                        for k in range(n_k):
                            ins = nc.tensor.matmul(acc[:, j, :], lhs_t(k, j), rhs(k), start=(k == 0),
                                                   stop=(k == n_k - 1))
                    ins.then_inc(acc_full, 1)

            def qkv(n):
                p = n % 2
                if n == 0:
                    pe.wait_ge(wqkv_halves, 2)
                pe.wait_ge(xn_low_a, KC * (n + 1))
                terms = [(kc, hw, hx) for kc in range(KC) for hw, hx in PASSES]
                for s in range(4):
                    project(4 * n + s, n, lambda t: wqkv_r[:, terms[t][1], terms[t][0], s * P:(s + 1) * P],
                            lambda t: xn_r[:, terms[t][2], p, terms[t][0], :], CHUNK, len(terms))
                    if n == NCH - 1:
                        attention(SELF, S1, SELF_EARLY[s], SELF_EARLY[s + 1])
                rows_product(("v", n), lambda t, j: xn_r[:, terms[t][2], p, terms[t][0], j * P:(j + 1) * P],
                             lambda t: wqkv_r[:, terms[t][1], terms[t][0], 2 * C:3 * C], len(terms))

            def context():
                pe.wait_ge(ctx_in, 32)
                for hh in range(2):
                    project(U_KC + hh, 0, lambda kc: wctx[:, kc, hh * P:(hh + 1) * P], lambda kc: ctxt[:, kc, :],
                            B * S_CTX)
                i = a_at["vc", 0]
                pe.wait_ge(acc_read, 2 * i)
                pe.wait_ge(split_a, 2 * U_QC)
                for b in range(B):
                    for kc in range(KC):
                        ins = nc.tensor.matmul(acc[0:S_CTX, 2 * b, :], ctxt[:, kc, b * S_CTX:(b + 1) * S_CTX],
                                               wctx[:, kc, C:2 * C], start=(kc == 0), stop=(kc == KC - 1))
                    ins.then_inc(acc_full, 1)

            def attention(a, s, lo, hi=None):
                def k_rows(n, g, h, lo, hi):
                    return (k_self[0:n, g % a.nb, h, lo:hi] if a.causal else k_ctx[0:n, g, h, lo:hi])

                def chunk(use, g, c):
                    t, h0, nh, s0, w = a.chunks[c]
                    if c == 0:
                        pe.wait_ge(s.q_in[g % a.nb], 16 * len(QP) * (1 + a.causal) * (g // a.nb + 1))
                        if g == 0 and not a.causal:
                            pe.wait_ge(s.k_in, 16 * len(KP))
                    diagonal = a.causal and s0 + w == (t + 1) * P
                    for h in range(h0, h0 + nh):
                        o = (h - h0) * w
                        ins = nc.tensor.matmul(m_bank(use)[:, o:o + w],
                                               q_stack[0:ROWS, g % a.nb, h, t * P:(t + 1) * P],
                                               k_rows(ROWS, g, h, s0, s0 + w), start=True, stop=not diagonal)
                        if diagonal:
                            ins = nc.tensor.matmul(m_bank(use)[:, o + w - P:o + w], identb[:, :], maskb[:, :],
                                                   start=False, stop=True)
                    return ins

                def shift_rows(use, g):
                    pe.wait_ge(s.shift_step, 5 * (g + 1))
                    dst = m_bank(use).bitcast(BF16)[0:PARTS * GH * TILES, 0:P]
                    return nc.tensor.transpose(dst, shift[:, :, :].rearrange("p a b -> p (a b)"), identb[:, :])

                def rows(use, n, half):
                    pe.wait_ge(s.heads_done, KC)
                    if a.causal and n == 0:
                        pe.wait_ge(mid_in, 16)
                    w0 = W1 if a.causal else W2
                    for j in range(2):
                        t0 = n * CHUNK + (2 * half + j) * P
                        for kc in range(KC):
                            ins = nc.tensor.matmul(m_bank(use)[:, j * C:(j + 1) * C], heads_out[:, kc, t0:t0 + P],
                                                   wmid[:, kc, w0:w0 + C], start=(kc == 0), stop=(kc == KC - 1))
                    return ins

                def score(g, u):
                    ui, h, k = a.units[u]
                    unit = len(a.units) * g + u
                    if u == 0:
                        pe.wait_ge(s.shift_in[g % a.nb], 16 * PARTS * (g // a.nb + 1))
                    at_least(pe, s.exps, unit - S_BANKS + 1)
                    for i, q0, w, off in a.steps[ui][0]:
                        lo, hi = max(off, k * BANK), min(off + w, (k + 1) * BANK)
                        if lo < hi:
                            keys = min(P, a.keys - i * P)
                            ins = nc.tensor.matmul(ps[0:keys, unit % S_BANKS, lo - k * BANK:hi - k * BANK],
                                                   k_rows(ROWS_S, g, h, i * P, i * P + keys),
                                                   q_stack[:, g % a.nb, h, q0 + lo - off:q0 + hi - off],
                                                   start=True, stop=True)
                    ins.then_inc(s.scores, 1)

                def product(g, ui):
                    if a.causal:
                        pe.wait_ge(s.masked, a.masks(g, ui))
                    else:
                        pe.wait_ge(s.exps, a.unit_index(g, ui + 1))
                    if ui == 0:
                        pe.wait_ge(s.v_set, g + 1 if a.causal else 1)
                        at_least(pe, s.out_copied, g)
                    slot = a.probs_slot(g, ui)
                    for i, q0, w, off in a.steps[ui][0]:
                        for bank in range(2):
                            lo, hi = max(q0, BANK * bank), BANK * (bank + 1)
                            if lo >= hi:
                                continue
                            last = i == a.kt - 1 or a.causal and bank == 0 and i == 3
                            for h in range(GH):
                                v = v_group[0:a.kp, g % 3, i, h, :] if a.causal else v_group[0:a.kp, 0, g, h, :]
                                o = off + lo - q0
                                ins = nc.tensor.matmul(out_region[32 * h:32 * h + 32, lo:hi], v,
                                                       probs[0:a.kp, slot, h, o:o + hi - lo],
                                                       start=(i == 0), stop=last, skip_group_check=True)
                    ins.then_inc(s.pv, 1)

                for op, *what in a.pe[lo:hi]:
                    if op == "score":
                        score(*what)
                    elif op == "product":
                        product(*what)
                    elif op == "m":
                        use = what[0]
                        kind, *of = a.uses[use]
                        at_least(pe, s.max_read, use - M_BANKS + 1)
                        {"chunk": chunk, "shift": shift_rows, "rows": rows}[kind](use, *of)\
                            .then_inc(s.max_full, 1)

            pe.wait_ge(consts, 7)
            for k in range(NCH):
                turn_norm(k)
                if k:
                    qkv(k - 1)
            attention(SELF, S1, 0, SELF_EARLY[0])
            qkv(NCH - 1)
            attention(SELF, S1, SELF_EARLY[4], SELF_EARLY[5])
            context()
            attention(SELF, S1, SELF_EARLY[5], SELF_EARLY[6])
            pe.wait_ge(split_a, 2 * U_QC)
            pe.wait_ge(acc_read, 2 * a_at["vc", 0] + 2)
            pe.wait_ge(consts, 9)
            attention(SELF, S1, SELF_EARLY[6])
            pe.wait_ge(S1.max_read, len(SELF.uses))
            pe.wait_ge(S1.exps, NG * len(SELF.units))

            def heads_product(k, s, w0):
                b, t0 = k % NCH // 2, k % 2 * CHUNK
                pe.wait_ge(s.heads_done, KC * (b + 1))
                rows_product(("w", k), lambda kc, j: heads_out[:, KC * b + kc, t0 + j * P:t0 + (j + 1) * P],
                             lambda kc: wmid[:, kc, w0:w0 + C], KC)

            def qc(n):
                k = NCH + n
                pe.wait_ge(tp_read, 2 * k + 2)
                for hh in range(2):
                    project(U_QC + 2 * n + hh, k, lambda kc: wmid[:, kc, WQ_C + hh * P:WQ_C + (hh + 1) * P],
                            lambda kc: xn_t[:, k % 2, kc, :], CHUNK)

            turn_norm(NCH)
            turn_norm(NCH + 1)
            pe.wait_ge(S1.out_copied, NG)
            qc(0)
            qc(1)
            heads_product(NCH + 2, S1, W1)
            heads_product(NCH + 3, S1, W1)
            turn_norm(NCH + 2)
            qc(2)
            attention(CROSS, S2, 0, CROSS_EARLY[0])
            turn_norm(NCH + 3)
            attention(CROSS, S2, CROSS_EARLY[0], CROSS_EARLY[1])
            qc(3)
            pe.wait_ge(split_a, 2 * U_H)
            attention(CROSS, S2, CROSS_EARLY[1], -1)
            pe.wait_ge(S2.exps, NG * len(CROSS.units))
            turn_norm(2 * NCH)
            attention(CROSS, S2, -1)
            pe.wait_ge(S2.max_read, len(CROSS.uses))
            pe.wait_ge(wf1_halves, 2)

            def feed_out(n):
                pe.wait_ge(hid_low, (FF // P) * (n + 1))
                if n == 0:
                    pe.wait_ge(wf2_halves, 2)
                    pe.wait_ge(S2.out_copied, NG)
                terms = [(k, hw, hx) for k in range(FF // P) for hx, hw in PASSES]
                rows_product(("f", n), lambda t, j: hid_r[:, terms[t][2], terms[t][0], j * P:(j + 1) * P],
                             lambda t: wf2r[:, terms[t][1], terms[t][0], :], len(terms))

            def hidden(n):
                k = 2 * NCH + n
                pe.wait_ge(xn_low, KC * (n + 1))
                for f in range(FF // P):
                    u = U_H + n * (FF // P) + f
                    ring_free(u)
                    terms = [(kc, hw, hx) for kc in range(KC) for hw, hx in PASSES]
                    for i, (kc, hw, hx) in enumerate(terms):
                        ins = nc.tensor.matmul(ps[:, 2 + u % 4, :], wf1r[hw][:, kc, f * P:(f + 1) * P],
                                               xn_r[:, hx, k % 2, kc, :], start=(i == 0),
                                               stop=(i == len(terms) - 1))
                    ins.then_inc(ring_full, 1)

            for n in range(NCH):
                hidden(n)
                if n + 1 < NCH:
                    turn_norm(2 * NCH + n + 1)
                feed_out(n)
                if n + 2 < NCH:
                    heads_product(2 * NCH + n + 2, S2, W2)

        @block.vector
        def _(dve):
            def ln_sums(k):
                n, p = k % NCH, k % 2
                at_least(dve, ln_var, k)
                at_least(dve, ln_done, CT * (k - 1))
                for j in range(CT):
                    nc.vector.bn_stats(stats[:, j, :], xs[:, n * CT + j, :]).then_inc(ln_stats, 1)
                dve.wait_ge(ln_stats, CT * (k + 1))
                for j in range(CT):
                    ins = nc.vector.bn_aggr(mean_var[:, p, j, :], stats[:, j, :])
                ins.then_inc(ln_var, 1)

            def ln_apply(k):
                n, p = k % NCH, k % 2
                dve.wait_ge(ln_rstd, k + 1)
                if 2 <= k < NCH or NCH + 2 <= k < 2 * NCH or 2 * NCH + 2 <= k:
                    dve.wait_ge(tp_full, 2 * (k - 2) + 2)
                for j in range(CT):
                    nc.vector.tensor_scalar(xn[:, p, j, :], xs[:, n * CT + j, :], mean_var[:, p, j, 0:1],
                                            rstd[:, p, j:j + 1], ALU.subtract, ALU.mult).then_inc(ln_done, 1)

            def split(u):
                width, _, _ = split_unit(u)
                p, f = parts[:, u % 4, :, 0:width], full[:, u % 2, 0:width]
                r = rest[:, u % 2, 0:width]
                dve.wait_ge(split_a, 2 * u + 2)
                at_least(dve, split_p, u - 1)
                nc.vector.tensor_tensor(r, f, p[:, 0, :], ALU.subtract).then_inc(split_v, 1)
                dve.wait_ge(split_v, 2 * u + 1)
                nc.vector.tensor_copy(p[:, 1, :], r).then_inc(split_v, 1)

            def add_v(n):
                b, i0 = n // 2, (n % 2) * CT
                for half in range(2):
                    dve.wait_ge(acc_full, 2 * a_at["v", n] + half + 1)
                    for j in (2 * half, 2 * half + 1):
                        dst = v_self[:, 4 * b:4 * b + 4, i0 + j, :]
                        ins = nc.vector.tensor_tensor(dst, acc[:, j, :].rearrange("p (g c) -> p g c", g=4),
                                                      row[:, BV_S, :].rearrange("p (g c) -> p g c", g=4), ALU.add)
                    ins.then_inc(acc_read, 1)

            def add_half(bank, n, half):
                xt = xs[:, n * CT + 2 * half:n * CT + 2 * half + 2, :]
                return nc.vector.tensor_tensor(xt, bank, xt, ALU.add)

            def add_rows(key, n, bias_k):
                i = a_at[key]
                dve.wait_ge(bias_added, bias_k + 1)
                for half in range(2):
                    dve.wait_ge(acc_full, 2 * i + half + 1)
                    add_half(acc[:, 2 * half:2 * half + 2, :], n, half).then_inc(acc_read, 1)
                dve.wait_ge(acc_read, 2 * i + 2)

            def attention(a, s, lo, hi=None):
                def chunk(use, g, c):
                    t, h0, nh, s0, w = a.chunks[c]
                    p = g % 2
                    if c == 0:
                        at_least(dve, s.shift_step, 5 * (g - 2) + 1)
                        at_least(dve, s.maxima, g - 1)
                    dst = max_b[:, p, h0:h0 + nh, t - 4:t - 3] if s0 else max_a[:, p, h0:h0 + nh, t:t + 1]
                    nc.vector.tensor_reduce(dst, m_bank(use)[:, 0:nh * w].rearrange("p (h w) -> p h w", h=nh),
                                            AX.X, ALU.max).then_inc(s.max_read, 1)
                    if c + 1 == len(a.chunks):
                        dve.wait_ge(s.max_read, use + 1)
                        late = max_a[:, p, :, 4:8]
                        nc.vector.tensor_tensor(late, late, max_b[:, p, :, :] if a.causal else late, ALU.max)\
                            .then_inc(s.maxima, 1)

                def shift_rows(use, g):
                    if g:
                        dve.wait_ge(s.shift_in[(g - 1) % a.nb], 16 * PARTS * ((g - 1) // a.nb + 1))
                    src = m_bank(use).bitcast(BF16)[0:PARTS * GH * TILES, 0:P]
                    nc.vector.tensor_copy(shift_t[:, :], src).then_inc(s.max_read, 1)

                def rows(use, n, half):
                    norm = (NCH if a.causal else 2 * NCH) + n
                    dve.wait_ge(bias_added, norm - NCH + 1)
                    add_half(m_bank(use).rearrange("p (j c) -> p j c", c=C), n, half).then_inc(s.max_read, 1)
                    if half:
                        dve.wait_ge(s.max_read, use + 1)
                        ln_sums(norm)

                def invert_sums(g):
                    if g % 2 == 0:
                        return
                    dve.wait_ge(s.heads_in, 32 * (g // 2 + 1))
                    nc.vector.reciprocal(sums[:, :], sums[:, :]).then_inc(s.recips_done, 1)

                def divide_heads(g):
                    if g % 2 == 0:
                        return
                    dve.wait_ge(s.recips_in, 16 * (g // 2 + 1))
                    o = heads_out[:, g // 2, :]
                    nc.vector.tensor_tensor(o, o, recips[:, :], ALU.mult).then_inc(s.heads_done, 1)

                for op, *what in a.pe[lo:hi]:
                    if op == "score" and a.behind("inverted", *what) is not None:
                        invert_sums(a.behind("inverted", *what))
                    if op == "score" and a.behind("divided", *what) is not None:
                        divide_heads(a.behind("divided", *what))
                    if op == "norm":
                        ln_apply((NCH if a.causal else 2 * NCH) + what[0])
                    if op != "m":
                        continue
                    use = what[0]
                    kind, *of = a.uses[use]
                    dve.wait_ge(s.max_full, use + 1)
                    {"chunk": chunk, "shift": shift_rows, "rows": rows}[kind](use, *of)
                return invert_sums, divide_heads

            for n in range(3):
                dve.wait_ge(x_in[n], 16)
                ln_sums(n)
                ln_apply(n)
                if n == 0:
                    dve.wait_ge(wqkv_halves, 1)
                    nc.vector.tensor_tensor(wqkv_r[:, LO], wqkv, wqkv_r[:, HI], ALU.subtract)\
                        .then_inc(wqkv_halves, 1)
            dve.wait_ge(row_in, 16)
            for n in range(3):
                for u in range(4):
                    split(4 * n + u)
                add_v(n)
                if n == 0:
                    dve.wait_ge(x_in[3], 16)
                    ln_sums(3)
                    ln_apply(3)
            attention(SELF, S1, 0, SELF_EARLY[0])
            for u in range(4):
                attention(SELF, S1, SELF_EARLY[u], SELF_EARLY[u + 1])
                split(4 * (NCH - 1) + u)
            add_v(NCH - 1)
            attention(SELF, S1, SELF_EARLY[4], SELF_EARLY[5])
            for u in range(2):
                split(U_KC + u)
            for b in range(B):
                dve.wait_ge(acc_full, 2 * a_at["vc", 0] + b + 1)
                nc.vector.tensor_tensor(v_ctx[:, 4 * b:4 * b + 4, :],
                                        acc[0:S_CTX, 2 * b, :].rearrange("p (g c) -> p g c", g=4),
                                        row[0:S_CTX, BV_C, :].rearrange("p (g c) -> p g c", g=4), ALU.add)\
                    .then_inc(acc_read, 1)
            invert_sums, divide_heads = attention(SELF, S1, SELF_EARLY[5])
            dve.wait_ge(S1.pv, SELF.n_steps * NG)
            split(U_QC)
            invert_sums(NG - 1)
            for u in range(1, 4):
                split(U_QC + u)
            divide_heads(NG - 1)
            for n in range(2, NCH):
                add_rows(("w", NCH + n), n, n)
                ln_sums(NCH + n)
                ln_apply(NCH + n)
            for u in range(4, 6):
                split(U_QC + u)
            attention(CROSS, S2, 0, CROSS_EARLY[1])
            for u in range(6, 8):
                split(U_QC + u)
            invert_sums, divide_heads = attention(CROSS, S2, CROSS_EARLY[1])

            def xn_low_half(n):
                k = 2 * NCH + n
                for kc in range(KC):
                    dve.wait_ge(tp_read, 2 * k + kc + 1)
                    nc.vector.tensor_tensor(xn_r[:, LO, k % 2, kc, :], xn_t[:, k % 2, kc, :],
                                            xn_r[:, HI, k % 2, kc, :], ALU.subtract).then_inc(xn_low, 1)

            def hidden_low_halves(n, fs):
                for f in fs:
                    u = n * (FF // P) + f
                    dve.wait_ge(hid_done, u + 1)
                    nc.vector.tensor_tensor(hid_r[:, LO, f, :], full[:, (U_H + u) % 2, :], hid_r[:, HI, f, :],
                                            ALU.subtract).then_inc(hid_low, 1)

            if NG - 3 in CROSS.left("inverted"):
                invert_sums(NG - 3)
            xn_low_half(0)
            for n in range(NCH):
                if n == 0:
                    hidden_low_halves(n, range(0, 1))
                    divide_heads(NG - 3)
                    hidden_low_halves(n, range(1, 4))
                    invert_sums(NG - 1)
                    hidden_low_halves(n, range(4, FF // P))
                    divide_heads(NG - 1)
                elif n + 1 < NCH:
                    add_rows(("w", 2 * NCH + n + 1), n + 1, NCH + n + 1)
                    ln_sums(2 * NCH + n + 1)
                    hidden_low_halves(n, range(0, 4))
                    ln_apply(2 * NCH + n + 1)
                    hidden_low_halves(n, range(4, FF // P))
                else:
                    hidden_low_halves(n, range(FF // P))
                if n + 1 < NCH:
                    xn_low_half(n + 1)
                add_rows(("f", n), n, 2 * NCH + n)


def kernel(x, ctx_1024, **w):
    import numpy as np
    import concourse.bacc as bacc
    from concourse.bass_utils import run_bass_kernel_spmd as run

    w = {k.removeprefix("L0_xattn_"): np.asarray(v) for k, v in w.items()}

    def flat(name):
        return w[name].transpose(1, 0, 2).reshape(C, H * D)

    def channel_cols(v):
        return v.reshape(-1, P).T

    arrays = {
        "x": np.asarray(x),
        "w_qkv": np.concatenate([flat("Wq_s"), flat("Wk_s"), flat("Wv_s")], 1),
        "w_ctx": np.concatenate([flat("Wk_c"), flat("Wv_c")], 1),
        "w_mid": np.concatenate([w["W1"], flat("Wq_c"), w["W2"]], 1),
        "w_f1": w["Wf1"],
        "w_f2": w["Wf2"],
        "ctx_t": np.asarray(ctx_1024).reshape(B * S_CTX, C).T,
        "cols": np.concatenate([channel_cols(w[k]) for k in
                                ("bq_s", "bk_s", "bq_c", "bk_c", "g1", "be1", "g2", "be2", "g3", "be3", "bf1")], 1),
        "rows": np.stack([w[k].reshape(C) for k in ("bv_s", "b1", "bv_c", "b2", "bf2")]),
    }
    arrays = {k: np.ascontiguousarray(v) for k, v in arrays.items()}
    nc = bacc.Bacc("TRN2", target_bir_lowering=False, num_devices=1)
    args = [nc.dram_tensor(f"in_{k}", v.shape, mybir.dt.from_np(v.dtype), kind="ExternalInput").ap()
            for k, v in arrays.items()]
    out = nc.dram_tensor("out", (B, T, C), F32, kind="ExternalOutput").ap()
    build(nc, *args, out)
    r = run(nc, [{f"in_{k}": v for k, v in arrays.items()}], core_ids=[0])
    return r.results[0]["out"]
```
